# Optimizing a Trainium2 kernel written in Bass

```python
import numpy as np
import jax
import jax.numpy as jnp

def _softmax(x, axis=-1):
    return jax.nn.softmax(x, axis=axis)

def _gelu(x):
    return jax.nn.gelu(x, approximate=True)

def _silu(x):
    return jax.nn.silu(x)

def _sigmoid(x):
    return jax.nn.sigmoid(x)

def _layernorm(x, axis=-1, eps=1e-05):
    m = jnp.mean(x, axis=axis, keepdims=True)
    v = jnp.var(x, axis=axis, keepdims=True)
    return (x - m) / jnp.sqrt(v + eps)

def _scatter_add(tgt, idx, src, axis=0):
    return tgt.at[idx].add(src)

def _segment_sum(src, seg, n):
    return jax.ops.segment_sum(src, seg, n)
kernel_name = 'mk_xattn_ffn_d4_seqx_r8_2d1d85'

def setup_inputs(seed: int=0):
    np.random.seed(seed)
    _w = jnp.asarray

    def _rec_inputs():
        import jax
        import jax.numpy as jnp
        _rk = jax.random.key(seed)
        x = -0.0003929 + 0.9999 * jax.random.normal(jax.random.fold_in(_rk, 1), (16, 64, 512), jnp.float32)
        _lenS = 64 - jax.random.randint(jax.random.fold_in(_rk, 7), (16,), 0, max(1, 64 // 4) + 1, jnp.int32)
        _lenS2 = 64 - jax.random.randint(jax.random.fold_in(_rk, 8), (16,), 0, max(1, 64 // 4) + 1, jnp.int32)
        _ctx_4096P = jax.random.normal(jax.random.fold_in(_rk, 11), (16, 16, 512), jnp.float32)
        _ctx_4096c = jax.random.dirichlet(jax.random.fold_in(_rk, 511), 0.3 * jnp.ones((16,), jnp.float32), (16, 64))
        _ctx_4096t = jnp.einsum('bsk,bkd->bsd', _ctx_4096c, _ctx_4096P)
        _ctx_4096t = _ctx_4096t * jax.lax.rsqrt(jnp.mean(jnp.square(_ctx_4096t)) + 1e-12) * 0.953939
        ctx_4096 = -5.78663e-05 + 0.999831 * (_ctx_4096t + 0.3 * jax.random.normal(jax.random.fold_in(_rk, 611), (16, 64, 512), jnp.float32))
        _validS = jnp.arange(64)[None, :] < _lenS[:, None]
        _validS2 = jnp.arange(64)[None, :] < _lenS2[:, None]
        _causal = jnp.tril(jnp.ones((64, 64), dtype=bool))
        mask_BxSxS2_ff0 = jnp.where(jnp.ones((16, 64, 64), dtype=bool), 0.0, -1000000000.0).astype(jnp.float32)
        mask_1x1xSxS2_ff0 = jnp.where(jnp.ones((1, 1, 64, 64), dtype=bool), 0.0, -1000000000.0).astype(jnp.float32)
        return (x, ctx_4096, mask_BxSxS2_ff0, mask_1x1xSxS2_ff0)
    x, ctx_4096, mask_BxSxS2_ff0, mask_1x1xSxS2_ff0 = _rec_inputs()

    def _L0_xattn_setup():
        import jax, jax.numpy as jnp
        import numpy as np
        EPS = 1e-06

        def rmsnorm(x, w):
            xf = x.astype(jnp.float32)
            var = jnp.mean(xf * xf, axis=-1, keepdims=True)
            return (xf * jax.lax.rsqrt(var + EPS)).astype(x.dtype) * w
        key = jax.random.key(seed)
        ks = jax.random.split(key, 6)
        B, T, S, Dt, Df = (4, 128, 72, 512, 512)
        text = jax.random.normal(ks[0], (B, T, Dt), dtype=jnp.float32)
        features = jax.random.normal(ks[1], (B, S, Df), dtype=jnp.float32)
        lim_q = float(np.sqrt(6.0 / (Dt + Df)))
        lim_k = float(np.sqrt(6.0 / (Df + Df)))
        Wq_w = jax.random.uniform(ks[2], (Df, Dt), minval=-lim_q, maxval=lim_q, dtype=jnp.float32)
        Wk_w = jax.random.uniform(ks[3], (Df, Df), minval=-lim_k, maxval=lim_k, dtype=jnp.float32)
        bq = 1.0 / np.sqrt(Dt)
        bk = 1.0 / np.sqrt(Df)
        Wq_b = jax.random.uniform(ks[4], (Df,), minval=-bq, maxval=bq, dtype=jnp.float32)
        Wk_b = jax.random.uniform(ks[5], (Df,), minval=-bk, maxval=bk, dtype=jnp.float32)
        fn_w = jnp.ones((Df,), dtype=jnp.float32)
        qn_w = jnp.ones((Df,), dtype=jnp.float32)
        kn_w = jnp.ones((Df,), dtype=jnp.float32)
        return {'text': text, 'features': features, 'Wq_w': Wq_w, 'Wq_b': Wq_b, 'Wk_w': Wk_w, 'Wk_b': Wk_b, 'fn_w': fn_w, 'qn_w': qn_w, 'kn_w': kn_w}
    _L0_xattn_all = _L0_xattn_setup()
    _L0_xattn_in = {k: v for k, v in _L0_xattn_all.items() if k in ('Wq_w', 'Wq_b', 'Wk_w', 'Wk_b', 'fn_w', 'qn_w', 'kn_w')}
    del _L0_xattn_all

    def _L0_ffn_setup():
        import jax, jax.numpy as jnp
        import numpy as np
        N_EXPERTS = 28
        TOP_K = 2
        RANK = 8
        LORA_ALPHA = 16
        SCALING = LORA_ALPHA / RANK
        TEMP = 1.0
        key = jax.random.key(seed)
        ks = jax.random.split(key, 5)
        B, S, D_IN, D_OUT = (4, 256, 512, 512)
        x = jax.random.normal(ks[0], (B, S, D_IN), dtype=jnp.float32)
        base_W = jax.random.normal(ks[1], (D_OUT, D_IN), dtype=jnp.float32) * (1.0 / np.sqrt(D_IN))
        gate_W = jax.random.normal(ks[2], (N_EXPERTS, D_IN), dtype=jnp.float32) * (1.0 / np.sqrt(D_IN))
        lora_A = jax.random.normal(ks[3], (N_EXPERTS, RANK, D_IN), dtype=jnp.float32) * (1.0 / np.sqrt(D_IN))
        lora_B = jax.random.normal(ks[4], (N_EXPERTS, D_OUT, RANK), dtype=jnp.float32) * 0.01
        return {'x': x, 'base_W': base_W, 'gate_W': gate_W, 'lora_A': lora_A, 'lora_B': lora_B}
    _L0_ffn_all = _L0_ffn_setup()
    _L0_ffn_in = {k: v for k, v in _L0_ffn_all.items() if k in ('base_W', 'gate_W', 'lora_A', 'lora_B')}
    del _L0_ffn_all

    def _L1_xattn_setup():
        import jax, jax.numpy as jnp
        import numpy as np
        B, S, D = (4, 128, 512)
        HQ, HKV, DK, DV = (32, 8, 128, 128)

        def apply_rope(x, positions):
            d = x.shape[-1]
            inv_freq = 1.0 / 10000.0 ** (jnp.arange(0, d, 2, dtype=jnp.float32) / d)
            ang = positions.astype(jnp.float32)[:, None] * inv_freq[None, :]
            cos = jnp.cos(ang)[None, None]
            sin = jnp.sin(ang)[None, None]
            x1, x2 = (x[..., :d // 2], x[..., d // 2:])
            return jnp.concatenate([x1 * cos - x2 * sin, x2 * cos + x1 * sin], axis=-1)
        key = jax.random.key(seed)
        ks = jax.random.split(key, 8)
        return {'query': jax.random.normal(ks[0], (B, S, D), jnp.float32), 'key': jax.random.normal(ks[1], (B, S, D), jnp.float32), 'value': jax.random.normal(ks[2], (B, S, D), jnp.float32), 'mask': jnp.zeros((B, S, S), jnp.float32), 'wq': jax.random.normal(ks[3], (D, HQ * DK), jnp.float32) * 0.02, 'wk': jax.random.normal(ks[4], (D, HKV * DK), jnp.float32) * 0.02, 'wv': jax.random.normal(ks[5], (D, HKV * DV), jnp.float32) * 0.02, 'wo': jax.random.normal(ks[6], (HQ * DV, D), jnp.float32) * 0.02, 'curr_seq_pos': 0}
    _L1_xattn_all = _L1_xattn_setup()
    _L1_xattn_in = {k: v for k, v in _L1_xattn_all.items() if k in ('wq', 'wk', 'wv', 'wo')}
    del _L1_xattn_all

    def _L1_ffn_setup():
        import jax, jax.numpy as jnp
        import numpy as np

        def _block_dequantize_mixed(packed, scale, mask):
            q_lo = packed & 15
            q_hi = packed >> 4 & 15
            q = jnp.stack([q_lo, q_hi], axis=-1).reshape(packed.shape[0], -1)
            scale_eff = scale.astype(jnp.float32) * jnp.where(mask[:, None], 1.0, 0.5)
            return (q.astype(jnp.float32) - 8.0) * scale_eff
        key = jax.random.key(seed)
        k1, k2, k3, k4, k5 = jax.random.split(key, 5)
        B, S, IN, OUT, G = (8, 256, 512, 512, 32)
        NB = OUT * IN // G
        x = jax.random.normal(k1, (B, S, IN), dtype=jnp.float32)
        weight_packed = jax.random.randint(k2, (NB, G // 2), 0, 32, dtype=jnp.int32)
        weight_scale = (jax.random.uniform(k3, (NB, 1)) * 0.02).astype(jnp.float16)
        weight_var_mask = jax.random.randint(k4, (NB,), 0, 2) > 0
        bias = jax.random.normal(k5, (OUT,), dtype=jnp.float32)
        return {'x': x, 'weight_packed': weight_packed, 'weight_scale': weight_scale, 'weight_var_mask': weight_var_mask, 'bias': bias}
    _L1_ffn_all = _L1_ffn_setup()
    _L1_ffn_in = {k: v for k, v in _L1_ffn_all.items() if k in ('weight_packed', 'weight_scale', 'weight_var_mask', 'bias')}
    del _L1_ffn_all

    def _L2_xattn_setup():
        import jax, jax.numpy as jnp
        import numpy as np
        B, Q, K, D = (1, 128, 6404, 512)
        H, KVH, HD = (32, 8, 128)
        GROUPS = H // KVH
        EPS = 1e-05

        def _rmsnorm(x, w):
            xf = x.astype(jnp.float32)
            var = jnp.mean(xf * xf, axis=-1, keepdims=True)
            return (xf * jax.lax.rsqrt(var + EPS)).astype(x.dtype) * w
        key = jax.random.key(seed)
        ks = jax.random.split(key, 8)
        s = 0.02
        return {'hidden_states': jax.random.normal(ks[0], (B, Q, D), jnp.float32), 'cross_attention_states': jax.random.normal(ks[1], (B, K, D), jnp.float32), 'attention_mask': jnp.zeros((B, 1, Q, K), jnp.float32), 'Wq': jax.random.normal(ks[2], (H * HD, D), jnp.float32) * s, 'Wk': jax.random.normal(ks[3], (KVH * HD, D), jnp.float32) * s, 'Wv': jax.random.normal(ks[4], (KVH * HD, D), jnp.float32) * s, 'Wo': jax.random.normal(ks[5], (D, H * HD), jnp.float32) * s, 'q_norm_w': jnp.ones((HD,), jnp.float32), 'k_norm_w': jnp.ones((HD,), jnp.float32)}
    _L2_xattn_all = _L2_xattn_setup()
    _L2_xattn_in = {k: v for k, v in _L2_xattn_all.items() if k in ('Wq', 'Wk', 'Wv', 'Wo', 'q_norm_w', 'k_norm_w')}
    del _L2_xattn_all

    def _L2_ffn_setup():
        import jax, jax.numpy as jnp
        import numpy as np
        LORA_SCALE = 16.0 / jnp.sqrt(16.0)
        TOP_K = 2
        key = jax.random.key(seed)
        k1, k2, k3, k4 = jax.random.split(key, 4)
        B_, S, D, O, E, R = (4, 256, 512, 512, 4, 16)
        x = jax.random.normal(k1, (B_, S, D), dtype=jnp.float32)
        router_w = jax.random.normal(k2, (E, D), dtype=jnp.float32) * 0.02
        A = jax.random.normal(k3, (E, R, D), dtype=jnp.float32) * 0.02
        B = jax.random.normal(k4, (O,), dtype=jnp.float32)
        B = jax.random.normal(k4, (E, O, R), dtype=jnp.float32) * 0.02
        return {'x': x, 'router_w': router_w, 'A': A, 'B': B}
    _L2_ffn_all = _L2_ffn_setup()
    _L2_ffn_in = {k: v for k, v in _L2_ffn_all.items() if k in ('router_w', 'A', 'B')}
    del _L2_ffn_all

    def _L3_xattn_setup():
        import jax, jax.numpy as jnp
        import numpy as np
        import math
        HIDDEN = 512
        N_HEADS = 32
        HEAD_DIM = 128
        N_KV_HEADS = 4
        N_GROUPS = N_HEADS // N_KV_HEADS
        key = jax.random.key(seed)
        ks = jax.random.split(key, 6)
        B, NL, S = (8, 64, 512)
        latents = jax.random.normal(ks[0], (B, NL, HIDDEN), dtype=jnp.float32)
        context = jax.random.normal(ks[1], (B, S, HIDDEN), dtype=jnp.float32)
        scale = 1.0 / math.sqrt(HIDDEN)
        Wq = jax.random.normal(ks[2], (HIDDEN, N_HEADS * HEAD_DIM), dtype=jnp.float32) * scale
        Wk = jax.random.normal(ks[3], (HIDDEN, N_KV_HEADS * HEAD_DIM), dtype=jnp.float32) * scale
        Wv = jax.random.normal(ks[4], (HIDDEN, N_KV_HEADS * HEAD_DIM), dtype=jnp.float32) * scale
        Wo = jax.random.normal(ks[5], (N_HEADS * HEAD_DIM, HIDDEN), dtype=jnp.float32) * scale
        return {'latents': latents, 'context': context, 'Wq': Wq, 'Wk': Wk, 'Wv': Wv, 'Wo': Wo}
    _L3_xattn_all = _L3_xattn_setup()
    _L3_xattn_in = {k: v for k, v in _L3_xattn_all.items() if k in ('Wq', 'Wk', 'Wv', 'Wo')}
    del _L3_xattn_all

    def _L3_ffn_setup():
        import jax, jax.numpy as jnp
        import numpy as np
        B, S, D, O, R, E = (4, 256, 512, 512, 16, 8)
        SCALING = 32.0 / 16.0
        key = jax.random.key(seed)
        ks = jax.random.split(key, 7)
        x = jax.random.normal(ks[0], (B, S, D), dtype=jnp.float32)
        W_base = jax.random.normal(ks[1], (O, D), dtype=jnp.float32) * 0.02
        b_base = jnp.zeros((O,), dtype=jnp.float32)
        A_w = jax.random.normal(ks[2], (R, D), dtype=jnp.float32) * 0.02
        B_w = jax.random.normal(ks[3], (O, R), dtype=jnp.float32) * 0.02
        router_w = jax.random.normal(ks[4], (E, D), dtype=jnp.float32) * 0.02
        cores = jax.random.normal(ks[5], (E, R, R), dtype=jnp.float32)
        return {'x': x, 'W_base': W_base, 'b_base': b_base, 'A_w': A_w, 'B_w': B_w, 'router_w': router_w, 'cores': cores}
    _L3_ffn_all = _L3_ffn_setup()
    _L3_ffn_in = {k: v for k, v in _L3_ffn_all.items() if k in ('W_base', 'b_base', 'A_w', 'B_w', 'router_w', 'cores')}
    del _L3_ffn_all
    return {'x': x, 'ctx_4096': ctx_4096, 'mask_BxSxS2_ff0': mask_BxSxS2_ff0, 'mask_1x1xSxS2_ff0': mask_1x1xSxS2_ff0, 'L0_xattn_Wq_w': _L0_xattn_in['Wq_w'], 'L0_xattn_Wq_b': _L0_xattn_in['Wq_b'], 'L0_xattn_Wk_w': _L0_xattn_in['Wk_w'], 'L0_xattn_Wk_b': _L0_xattn_in['Wk_b'], 'L0_xattn_fn_w': _L0_xattn_in['fn_w'], 'L0_xattn_qn_w': _L0_xattn_in['qn_w'], 'L0_xattn_kn_w': _L0_xattn_in['kn_w'], 'L0_ffn_base_W': _L0_ffn_in['base_W'], 'L0_ffn_gate_W': _L0_ffn_in['gate_W'], 'L0_ffn_lora_A': _L0_ffn_in['lora_A'], 'L0_ffn_lora_B': _L0_ffn_in['lora_B'], 'L1_xattn_wq': _L1_xattn_in['wq'], 'L1_xattn_wk': _L1_xattn_in['wk'], 'L1_xattn_wv': _L1_xattn_in['wv'], 'L1_xattn_wo': _L1_xattn_in['wo'], 'L1_ffn_weight_packed': _L1_ffn_in['weight_packed'], 'L1_ffn_weight_scale': _L1_ffn_in['weight_scale'], 'L1_ffn_weight_var_mask': _L1_ffn_in['weight_var_mask'], 'L1_ffn_bias': _L1_ffn_in['bias'], 'L2_xattn_Wq': _L2_xattn_in['Wq'], 'L2_xattn_Wk': _L2_xattn_in['Wk'], 'L2_xattn_Wv': _L2_xattn_in['Wv'], 'L2_xattn_Wo': _L2_xattn_in['Wo'], 'L2_xattn_q_norm_w': _L2_xattn_in['q_norm_w'], 'L2_xattn_k_norm_w': _L2_xattn_in['k_norm_w'], 'L2_ffn_router_w': _L2_ffn_in['router_w'], 'L2_ffn_A': _L2_ffn_in['A'], 'L2_ffn_B': _L2_ffn_in['B'], 'L3_xattn_Wq': _L3_xattn_in['Wq'], 'L3_xattn_Wk': _L3_xattn_in['Wk'], 'L3_xattn_Wv': _L3_xattn_in['Wv'], 'L3_xattn_Wo': _L3_xattn_in['Wo'], 'L3_ffn_W_base': _L3_ffn_in['W_base'], 'L3_ffn_b_base': _L3_ffn_in['b_base'], 'L3_ffn_A_w': _L3_ffn_in['A_w'], 'L3_ffn_B_w': _L3_ffn_in['B_w'], 'L3_ffn_router_w': _L3_ffn_in['router_w'], 'L3_ffn_cores': _L3_ffn_in['cores']}

def reference(x, ctx_4096, mask_BxSxS2_ff0, mask_1x1xSxS2_ff0, L0_xattn_Wq_w, L0_xattn_Wq_b, L0_xattn_Wk_w, L0_xattn_Wk_b, L0_xattn_fn_w, L0_xattn_qn_w, L0_xattn_kn_w, L0_ffn_base_W, L0_ffn_gate_W, L0_ffn_lora_A, L0_ffn_lora_B, L1_xattn_wq, L1_xattn_wk, L1_xattn_wv, L1_xattn_wo, L1_ffn_weight_packed, L1_ffn_weight_scale, L1_ffn_weight_var_mask, L1_ffn_bias, L2_xattn_Wq, L2_xattn_Wk, L2_xattn_Wv, L2_xattn_Wo, L2_xattn_q_norm_w, L2_xattn_k_norm_w, L2_ffn_router_w, L2_ffn_A, L2_ffn_B, L3_xattn_Wq, L3_xattn_Wk, L3_xattn_Wv, L3_xattn_Wo, L3_ffn_W_base, L3_ffn_b_base, L3_ffn_A_w, L3_ffn_B_w, L3_ffn_router_w, L3_ffn_cores):
    import jax
    import jax.numpy as jnp

    def _L0_xattn_ref(text, features, Wq_w, Wq_b, Wk_w, Wk_b, fn_w, qn_w, kn_w):
        import jax, jax.numpy as jnp
        import numpy as np
        EPS = 1e-06

        def rmsnorm(x, w):
            xf = x.astype(jnp.float32)
            var = jnp.mean(xf * xf, axis=-1, keepdims=True)
            return (xf * jax.lax.rsqrt(var + EPS)).astype(x.dtype) * w
        features_n = rmsnorm(features, fn_w)
        Q = jnp.einsum('btd,fd->btf', text, Wq_w) + Wq_b
        K = jnp.einsum('bsd,fd->bsf', features_n, Wk_w) + Wk_b
        Q = rmsnorm(Q, qn_w)
        K = rmsnorm(K, kn_w)
        scale = 1.0 / jnp.sqrt(jnp.asarray(K.shape[-1], dtype=Q.dtype))
        scores = jnp.einsum('btf,bsf->bts', Q, K) * scale
        attn = jax.nn.softmax(scores, axis=-1)
        attended = jnp.einsum('bts,bsf->btf', attn, features_n)
        return attended

    def _L0_ffn_ref(x, base_W, gate_W, lora_A, lora_B):
        import jax, jax.numpy as jnp
        import numpy as np
        N_EXPERTS = 28
        TOP_K = 2
        RANK = 8
        LORA_ALPHA = 16
        SCALING = LORA_ALPHA / RANK
        TEMP = 1.0
        B, S, D_in = x.shape
        xf = x.reshape(B * S, D_in)
        base = xf @ base_W.T
        logits = xf @ gate_W.T
        top_vals, top_idx = jax.lax.top_k(logits, TOP_K)
        top_probs = jax.nn.softmax(top_vals / TEMP, axis=-1)
        N = xf.shape[0]
        gate_full = jnp.zeros((N, N_EXPERTS), dtype=xf.dtype).at[jnp.arange(N)[:, None], top_idx].add(top_probs)
        h = jnp.einsum('nd,erd->ner', xf, lora_A)
        h = h * (gate_full * SCALING)[:, :, None]
        lora_out = jnp.einsum('ner,eor->no', h, lora_B)
        out = base + lora_out
        return out.reshape(B, S, -1)

    def _L1_xattn_ref(query, key, value, mask, wq, wk, wv, wo, curr_seq_pos):
        import jax, jax.numpy as jnp
        import numpy as np
        B, S, D = (4, 128, 512)
        HQ, HKV, DK, DV = (32, 8, 128, 128)

        def apply_rope(x, positions):
            d = x.shape[-1]
            inv_freq = 1.0 / 10000.0 ** (jnp.arange(0, d, 2, dtype=jnp.float32) / d)
            ang = positions.astype(jnp.float32)[:, None] * inv_freq[None, :]
            cos = jnp.cos(ang)[None, None]
            sin = jnp.sin(ang)[None, None]
            x1, x2 = (x[..., :d // 2], x[..., d // 2:])
            return jnp.concatenate([x1 * cos - x2 * sin, x2 * cos + x1 * sin], axis=-1)
        bs, sq, _ = query.shape
        sk = key.shape[1]
        n_groups = HQ // HKV
        q = (query @ wq).reshape(bs, sq, HQ, DK).transpose(0, 2, 1, 3)
        k = (key @ wk).reshape(bs, sk, HKV, DK)
        v = (value @ wv).reshape(bs, sk, HKV, DV)
        k = jnp.repeat(k, n_groups, axis=2).transpose(0, 2, 1, 3)
        v = jnp.repeat(v, n_groups, axis=2).transpose(0, 2, 1, 3)
        scale = jnp.sqrt(jnp.float32(DK))
        pos = curr_seq_pos + jnp.arange(sq)
        q = apply_rope(q, pos)
        k = apply_rope(k, curr_seq_pos + jnp.arange(sk))
        scores = jnp.einsum('bhqd,bhkd->bhqk', q, k) / scale
        m = jax.lax.dynamic_slice(mask, (0, curr_seq_pos, 0), (bs, sq, sk))
        attn = jax.nn.softmax(scores + m[:, None, :, :], axis=-1)
        out = jnp.einsum('bhqk,bhkd->bhqd', attn, v)
        out = out.transpose(0, 2, 1, 3).reshape(bs, sq, HQ * DV)
        return out @ wo

    def _L1_ffn_ref(x, weight_packed, weight_scale, weight_var_mask, bias):
        import jax, jax.numpy as jnp
        import numpy as np

        def _block_dequantize_mixed(packed, scale, mask):
            q_lo = packed & 15
            q_hi = packed >> 4 & 15
            q = jnp.stack([q_lo, q_hi], axis=-1).reshape(packed.shape[0], -1)
            scale_eff = scale.astype(jnp.float32) * jnp.where(mask[:, None], 1.0, 0.5)
            return (q.astype(jnp.float32) - 8.0) * scale_eff
        out_features = bias.shape[0]
        in_features = x.shape[-1]
        w = _block_dequantize_mixed(weight_packed, weight_scale, weight_var_mask)
        w = w.reshape(out_features, in_features)
        return jnp.einsum('bsi,oi->bso', x, w) + bias

    def _L2_xattn_ref(hidden_states, cross_attention_states, attention_mask, Wq, Wk, Wv, Wo, q_norm_w, k_norm_w):
        import jax, jax.numpy as jnp
        import numpy as np
        B, Q, K, D = (1, 128, 6404, 512)
        H, KVH, HD = (32, 8, 128)
        GROUPS = H // KVH
        EPS = 1e-05

        def _rmsnorm(x, w):
            xf = x.astype(jnp.float32)
            var = jnp.mean(xf * xf, axis=-1, keepdims=True)
            return (xf * jax.lax.rsqrt(var + EPS)).astype(x.dtype) * w
        bsz, q_len, _ = hidden_states.shape
        kv_len = cross_attention_states.shape[1]
        q = (hidden_states @ Wq.T).reshape(bsz, q_len, H, HD).transpose(0, 2, 1, 3)
        k = (cross_attention_states @ Wk.T).reshape(bsz, kv_len, KVH, HD).transpose(0, 2, 1, 3)
        v = (cross_attention_states @ Wv.T).reshape(bsz, kv_len, KVH, HD).transpose(0, 2, 1, 3)
        q = _rmsnorm(q, q_norm_w)
        k = jnp.repeat(k, GROUPS, axis=1)
        v = jnp.repeat(v, GROUPS, axis=1)
        k = _rmsnorm(k, k_norm_w)
        scale = 1.0 / np.sqrt(HD)
        scores = jnp.einsum('bhqd,bhkd->bhqk', q, k) * scale
        scores = scores + attention_mask[:, :, :, :kv_len]
        probs = jax.nn.softmax(scores.astype(jnp.float32), axis=-1).astype(q.dtype)
        out = jnp.einsum('bhqk,bhkd->bhqd', probs, v)
        out = out.transpose(0, 2, 1, 3).reshape(bsz, q_len, H * HD)
        return out @ Wo.T

    def _L2_ffn_ref(x, router_w, A, B):
        import jax, jax.numpy as jnp
        import numpy as np
        LORA_SCALE = 16.0 / jnp.sqrt(16.0)
        TOP_K = 2
        D = x.shape[-1]
        flat = x.reshape(-1, D)
        logits = flat @ router_w.T
        topk_vals, topk_idx = jax.lax.top_k(logits, TOP_K)
        sparse = jnp.full_like(logits, -jnp.inf)
        rows = jnp.arange(logits.shape[0])[:, None]
        sparse = sparse.at[rows, topk_idx].set(topk_vals)
        gates = jax.nn.softmax(sparse, axis=-1)
        mid = jnp.einsum('tf,erf->ter', flat, A)
        all_deltas = jnp.einsum('ter,eor->teo', mid, B) * LORA_SCALE
        delta = jnp.einsum('te,teo->to', gates, all_deltas)
        return delta.reshape(*x.shape[:-1], -1)

    def _L3_xattn_ref(latents, context, Wq, Wk, Wv, Wo):
        import jax, jax.numpy as jnp
        import numpy as np
        import math
        HIDDEN = 512
        N_HEADS = 32
        HEAD_DIM = 128
        N_KV_HEADS = 4
        N_GROUPS = N_HEADS // N_KV_HEADS
        b, q_len, _ = latents.shape
        kv_len = q_len + context.shape[1]
        hidden_states = jnp.concatenate([context, latents], axis=1)
        q = (latents @ Wq).reshape(b, q_len, N_KV_HEADS, N_GROUPS, HEAD_DIM)
        k = (hidden_states @ Wk).reshape(b, kv_len, N_KV_HEADS, HEAD_DIM)
        v = (hidden_states @ Wv).reshape(b, kv_len, N_KV_HEADS, HEAD_DIM)
        scale = 1.0 / math.sqrt(HEAD_DIM)
        scores = jnp.einsum('bqhgd,bkhd->bhgqk', q, k) * scale
        attn = jax.nn.softmax(scores.astype(jnp.float32), axis=-1).astype(q.dtype)
        out = jnp.einsum('bhgqk,bkhd->bqhgd', attn, v)
        out = out.reshape(b, q_len, N_HEADS * HEAD_DIM)
        return out @ Wo

    def _L3_ffn_ref(x, W_base, b_base, A_w, B_w, router_w, cores):
        import jax, jax.numpy as jnp
        import numpy as np
        B, S, D, O, R, E = (4, 256, 512, 512, 16, 8)
        SCALING = 32.0 / 16.0
        result = jnp.einsum('bsd,od->bso', x, W_base) + b_base
        ax = jnp.einsum('bsd,rd->bsr', x, A_w)
        probs = jax.nn.softmax(jnp.einsum('bsd,ed->bse', x, router_w), axis=-1)
        per_expert = jnp.einsum('bsr,erq->bseq', ax, cores)
        mixed = jnp.einsum('bseq,bse->bsq', per_expert, probs)
        result = result + jnp.einsum('bsr,or->bso', mixed, B_w) * SCALING
        return result
    x = x + _L0_xattn_ref(_layernorm(x, axis=-1), ctx_4096, L0_xattn_Wq_w, L0_xattn_Wq_b, L0_xattn_Wk_w, L0_xattn_Wk_b, L0_xattn_fn_w, L0_xattn_qn_w, L0_xattn_kn_w)
    x = x + _L0_ffn_ref(_layernorm(x, axis=-1), L0_ffn_base_W, L0_ffn_gate_W, L0_ffn_lora_A, L0_ffn_lora_B)
    x = x + _L1_xattn_ref(_layernorm(x, axis=-1), ctx_4096, ctx_4096, mask_BxSxS2_ff0, L1_xattn_wq, L1_xattn_wk, L1_xattn_wv, L1_xattn_wo, 0)
    x = x + _L1_ffn_ref(_layernorm(x, axis=-1), L1_ffn_weight_packed, L1_ffn_weight_scale, L1_ffn_weight_var_mask, L1_ffn_bias)
    x = x + _L2_xattn_ref(_layernorm(x, axis=-1), ctx_4096, mask_1x1xSxS2_ff0, L2_xattn_Wq, L2_xattn_Wk, L2_xattn_Wv, L2_xattn_Wo, L2_xattn_q_norm_w, L2_xattn_k_norm_w)
    x = x + _L2_ffn_ref(_layernorm(x, axis=-1), L2_ffn_router_w, L2_ffn_A, L2_ffn_B)
    x = x + _L3_xattn_ref(_layernorm(x, axis=-1), ctx_4096, L3_xattn_Wq, L3_xattn_Wk, L3_xattn_Wv, L3_xattn_Wo)
    x = x + _L3_ffn_ref(_layernorm(x, axis=-1), L3_ffn_W_base, L3_ffn_b_base, L3_ffn_A_w, L3_ffn_B_w, L3_ffn_router_w, L3_ffn_cores)
    return x

_drawn_inputs = setup_inputs


def setup_inputs(seed=0):
    import zlib

    import numpy as np

    out = dict(_drawn_inputs(seed))
    spreads = {'L0_xattn_fn_w': (1.0, 0.2),
     'L0_xattn_qn_w': (1.0, 0.577),
     'L0_xattn_kn_w': (1.0, 0.2),
     'L2_xattn_q_norm_w': (1.0, 0.6),
     'L2_xattn_k_norm_w': (1.0, 0.6),
     'L3_ffn_b_base': (0.0, 0.1)}
    factors = {'L0_xattn_Wq_b': 8.0,
     'L0_xattn_Wk_b': 8.0,
     'L0_ffn_gate_W': 3.057,
     'L0_ffn_lora_A': 2.917,
     'L0_ffn_lora_B': 2.944,
     'L1_xattn_wq': 5.665,
     'L1_xattn_wk': 5.66}
    for name, (base, spread) in spreads.items():
        noise = np.random.default_rng([zlib.crc32(name.encode()), seed]).standard_normal(out[name].shape)
        drawn = base * np.exp(spread * noise) if base else spread * noise
        out[name] = jnp.asarray(drawn.astype(out[name].dtype))
    for name, factor in factors.items():
        out[name] = (out[name] * factor).astype(out[name].dtype)
    return out
```

```python
from contextlib import ExitStack

import concourse.bass as bass
import numpy as np
from concourse import mybir

F32 = mybir.dt.float32
F32R = mybir.dt.float32r
F16 = mybir.dt.float16
I32 = mybir.dt.int32
U32 = mybir.dt.uint32
U8 = mybir.dt.uint8
ALU = mybir.AluOpType
ACT = mybir.ActivationFunctionType
AX_X = mybir.AxisListType.X

P = 128
B, S, D = 16, 64, 512
ROWS = B * S
TILES = ROWS // P
KC = D // P
HALVES = 2
HALF = ROWS // HALVES
HD = 128
HEADS = 32
GH = 4
UPW = 256
NEG = -1.0e30

C_ID, C_ONE, C_BLK, C_COS, C_SIN, C_IOTA, C_END = 0, 128, 256, 384, 448, 512, 544

GROUPS = HEADS // GH
W_L0Q, W_AG0, W_BASE0, W_L1Q = 0, 1, 2, 3
W_L1O = W_L1Q + 1
W_F1 = W_L1O + 2 * GROUPS - 1
W_L2Q = W_F1 + 1
W_L2O = W_L2Q + 1
W_AG2 = W_L2O + 2 * GROUPS - 1
W_L3Q = W_AG2 + 1
W_L3O = W_L3Q + 1
W_AG3 = W_L3O + 2 * GROUPS - 1
W_BASE3 = W_AG3 + 1
W_BLOCKS = W_BASE3 + 1
KV_BLOCKS = 8 + 8 + 4 + 1


class Layer:

    def __init__(self, name, subs, turns, w_o, kv):
        self.name, self.subs, self.turns = name, subs, turns
        self.w_o, self.kv = w_o, kv
        self.rope, self.norm, self.wide = name == "L1", name == "L2", name == "L3"
        self.keys = 2 * S if self.wide else S
        self.uses, self.pre, self.fill = [], [], []
        for sub in range(subs):
            q = [("q", sub, half, h) for half in range(HALVES) for h in range(GH)]
            wo = [("wo", sub, t) for t in range(TILES)]
            sq = lambda u: [("ss",) + u] if self.norm else []
            pre = []
            if sub == 0 and self.wide:
                pre = [("k", src, half) for half in range(HALVES) for src in range(2)]
                pre += [("v", 0, 0), ("v", 1, 0), q[0], ("vt", 0, 0), ("vt", 0, 1)]
                pre += [("v", 0, 1), ("v", 1, 1), q[1], ("vt", 1, 0), ("vt", 1, 1)]
                pre += [q[2], q[3], q[4]]
            elif sub == 0:
                pre = [("k", 0, 0), ("v", 0, 0), ("k", 0, 1), ("v", 0, 1)]
                pre += sq(("k", 0, 0)) + sq(("k", 0, 1))
                pre += [q[0], ("vt", 0, 0), ("vt", 1, 0), q[1]] + sq(q[0]) + [q[2]] + sq(q[1])
                pre += [q[3]] + sq(q[2]) + [q[4]] + sq(q[3])
            else:
                pre = q[0:5]
            fill = [[q[5]] + sq(q[4]), [q[6]] + sq(q[5]), [q[7]] + sq(q[6]), sq(q[7]) + [wo[0]]]
            fill += [[w] for w in wo[1:]]
            self.pre.append(pre)
            self.fill.append(fill)
            for u in pre + [x for f in fill for x in f]:
                self.uses.append(u)
        n = len(self.uses)
        self.bank_of = [i % 3 for i in range(n)]
        if n % 3 == 1:
            self.bank_of[-1] = 1
        self.n = n
        self.by_act = [u for u in self.uses if self.emptier(u) == "act"]
        self.by_dve = [u for u in self.uses if self.emptier(u) == "dve"]
        self.normed = [u for u in self.uses if u[0] == "ss"]
        self.roped = [u for u in self.uses if u[0] in "kq"]
        self.tiles = subs * TILES

    def emptier(self, use):
        if use[0] == "wo" or (self.rope and use[0] in "kq"):
            return "dve"
        return "act"

    def before(self, use):
        i = self.uses.index(use)
        for back in range(1, self.n + 1):
            if self.bank_of[(i - back) % self.n] == self.bank_of[i]:
                return self.uses[(i - back) % self.n], i - back < 0


L1 = Layer("L1", 1, 8, W_L1O, 0)
L2 = Layer("L2", 1, 8, W_L2O, 8)
L3 = Layer("L3", 2, 4, W_L3O, 16)


class Ffn:
    def __init__(self, name, base, bias, experts, rank, mix, scale):
        self.name, self.base, self.bias, self.experts, self.rank = name, base, bias, experts, rank
        self.mix, self.scale = mix, scale
        self.wide = experts * rank
        self.chunks = 2 if self.wide > P else 1
        self.chunk = self.wide // self.chunks if experts else 0
        self.out_lag = 4 if experts else 1
        self.add_lag = self.out_lag + 1
        self.next_lag = self.out_lag + 2


F0 = Ffn("F0", True, False, 28, 8, False, 2.0)
F1 = Ffn("F1", True, True, 0, 0, False, 1.0)
F2 = Ffn("F2", False, False, 4, 16, False, 4.0)
F3 = Ffn("F3", True, True, 8, 16, True, 2.0)

JOBS = [(what, t) for t in range(TILES) for what in ("ctx", 0, "feat")]
for phase_, f_ in ((1, F0), (3, F1), (5, F2), (7, F3)):
    for i_ in range(TILES + f_.next_lag):
        if i_ < TILES:
            JOBS.append((phase_, i_))
        if phase_ < 7 and 0 <= i_ - f_.next_lag:
            JOBS.append((phase_ + 1, i_ - f_.next_lag))
XN_ORDER = [job for job in JOBS if job[0] not in ("ctx", "feat")]
LN_ORDER = [(0, 0), (0, 1)]
for i_ in range(TILES + 3):
    LN_ORDER += [(0, i_ + 2)] if i_ + 2 < TILES else []
    LN_ORDER += [(1, i_ - 3)] if i_ >= 3 else []
LN_ORDER += [(phase_, t) for phase_ in range(2, 8) for t in range(TILES)]


def build(nc, a, out):
    with ExitStack() as ctx:
        def sb(name, cols, dt=F32):
            return ctx.enter_context(nc.sbuf_tensor(name, [P, cols], dt))

        def sem(name):
            return ctx.enter_context(nc.semaphore(name))

        ps = [ctx.enter_context(nc.psum_tensor(f"bank{i}", [P, 512], F32)) for i in range(8)]

        x_sb = sb("x_sb", TILES * D)
        x = x_sb[:, :].rearrange("p (t d) -> p t d", t=TILES)
        parts = {}
        for name in ("xT", "cT"):
            for part in ("hi", "lo"):
                parts[name, part] = sb(f"{name}_{part}", KC * ROWS, F32R)[:, :].rearrange("p (c r) -> p c r", c=KC)
        xT, cT = [[parts[n, p] for p in ("hi", "lo")] for n in ("xT", "cT")]
        w_raw = sb("w_raw", KC * D)
        wq_t = [sb(f"wq_{p}", KC * D, F32R) for p in ("hi", "lo")]
        wo_t = [sb(f"wo_{p}", KC * D, F32R) for p in ("hi", "lo")]
        wq = [w[:, :].rearrange("p (c n) -> p c n", c=KC) for w in wq_t]
        wo = [w[:, :].rearrange("p (c n) -> p c n", c=KC) for w in wo_t]
        kv_raw = sb("kv_raw", 2 * KC * HD)
        kv_t = [sb(f"kv_{p}", 2 * KC * HD, F32R) for p in ("hi", "lo")]
        wkv = [w[:, :].rearrange("p (s c n) -> p s c n", s=2, c=KC) for w in kv_t]
        q_sb = sb("q_sb", GH * ROWS)
        oT_t = [sb(f"oT_{p}", 4 * GH * P, F32R) for p in ("hi", "lo")]
        oT = [o[:, :].rearrange("p (s h r) -> p s h r", s=4, h=GH) for o in oT_t]
        k_sb = sb("k_sb", 2 * ROWS)
        vT_sb = sb("vT_sb", ROWS)
        v_sb = sb("v_sb", 2 * ROWS)
        s_sb = sb("s_sb", 2 * 512)
        pt_sb = sb("pt_sb", 2 * 512)
        m1_sb = sb("m1_sb", B * S)
        m2_sb = sb("m2_sb", S)
        tmp_sb = sb("tmp_sb", 2 * 512)
        cst = sb("cst", C_END)
        small = sb("small", 192)
        stats = sb("stats", TILES * 6)
        idx8 = sb("idx8", 8, U32)

        ident = cst[:, C_ID:C_ID + P]
        ones = cst[:, C_ONE:C_ONE + P]
        blk = cst[:, C_BLK:C_BLK + P]
        iota = cst[:, C_IOTA:C_IOTA + 32]
        qT = q_sb[:, :].rearrange("p (b h r) -> p b h r", b=B, h=GH)
        mv = small[:, 0:16].rearrange("p (t s) -> p t s", s=2)
        rstd = small[:, 16:24]
        feat_ss = small[:, 24:32]
        feat_r = small[:, 32:40]
        mx = small[:, 40:48].rearrange("p (b j) -> p b j", b=2)
        sm = small[:, 48:56].rearrange("p (b j) -> p b j", b=2)
        rc = small[:, 56:64].rearrange("p (b j) -> p b j", b=2)
        eps5, eps6 = small[:, 64:65], small[:, 65:66]
        qk_w = small[:, 66:74]
        qk_raw = small[:, 74:84]
        ss0 = small[:, 84:88].rearrange("p (b j) -> p b j", b=2)
        r0 = small[:, 88:92].rearrange("p (b j) -> p b j", b=2)
        lg = small[:, 92:124]
        top8 = small[:, 124:132]
        idxf = small[:, 132:134]
        gate_d, gate_e, gate_a, gate_r, gate_p = [small[:, 134 + i:136 + i - 1] for i in range(5)]
        gate_p2 = small[:, 139:140]
        g1 = small[:, 140:168]
        c_nat = q_sb[:, :].rearrange("p (t d) -> p t d", t=TILES)
        qk_rows = k_sb[:, :].rearrange("p (b s d) -> p b s d", b=2, s=2)
        bq_row, bk_row, fn_row, ctx_squares = [v_sb[:, i * D:(i + 1) * D] for i in range(4)]
        qk_squares = m1_sb[:, :].rearrange("p (s d) -> p s d", s=2)
        wk_raw = k_sb[:, :]
        QT0, KT0 = [vT_sb[:, i * D:(i + 1) * D].rearrange("p (c r) -> p c r", c=KC) for i in range(2)]
        up_w = k_sb[:, 0:2 * D].rearrange("p (c d) -> p c d", c=2)
        cores = k_sb[:, 2 * D:2 * D + 16]
        bias_row = v_sb[:, 0:D]
        hm = q_sb[:, 0:512].rearrange("p (b n) -> p b n", b=2)
        hT = q_sb[:, 512:1536].rearrange("p (b c r) -> p b c r", b=4, c=2)
        mT = q_sb[:, 1536:1792].rearrange("p (b r) -> p b r", b=2)
        xn = tmp_sb[:, :].rearrange("p (b d) -> p b d", b=2)
        packed = q_sb[:, 1536:2560].bitcast(I32)
        nib = q_sb[:, 2560:3584].bitcast(I32)
        scale16 = q_sb[:, 3584:4096].bitcast(F16)
        mask_words = k_sb[:, 1040:1296].bitcast(I32)
        mask8 = mask_words.bitcast(U8)
        nibf = [v_sb[:, i * ROWS:(i + 1) * ROWS] for i in range(2)]
        sc_f = vT_sb[:, :]

        s_const = sem("consts_loaded")
        s_eps = sem("eps_written")
        s_x = [sem(f"x_loaded_{t}") for t in range(TILES)]
        s_ctx = [sem(f"ctx_loaded_{t}") for t in range(TILES)]
        wk_loaded, wk_hi, wk_split = sem("wk_loaded"), sem("wk_hi"), sem("wk_split")
        s_mask = sem("masks_loaded")
        s_out = sem("out_stored")
        w_loaded, w_hi, w_split = sem("w_loaded"), sem("w_hi"), sem("w_split")
        kv_loaded, kv_hi, kv_split = sem("kv_loaded"), sem("kv_hi"), sem("kv_split")
        tr_full, tr_hi, tr_lo = sem("tr_full"), sem("tr_hi"), sem("tr_lo")
        ln_var, ln_tmp, ln_rstd, xn_ready = sem("ln_var"), sem("ln_tmp"), sem("ln_rstd"), sem("xn_ready")
        dve_step = sem("dve_step")
        act_step = sem("act_step")
        x_added = sem("x_added")
        extra_loaded = sem("extra_loaded")
        f1_loaded, f1_ready, f1_stored = sem("f1_loaded"), sem("f1_ready"), sem("f1_stored")

        z = {k: sem(f"L0_{k}") for k in ("ss_c r_c feat qk_full qb ss r qn qkt_full qkt_q qkt_k s_full s_read "
                                         "exp p_ready pt_full pt_ready av_full").split()}

        def layer_sems(lay):
            names = "full ev_act ev_dve s_full s_read s_max s_shift exp s_sum s_rec p_ready t_full pt_ready o_full o_hi o_lo"
            names += " roped" if lay.rope else ""
            names += " r_tmp r_ready normed" if lay.norm else ""
            made = {k: sem(f"{lay.name}_{k}") for k in names.split()}
            per = {k: lay.tiles for k in made}
            per.update(full=lay.n, ev_act=len(lay.by_act), ev_dve=len(lay.by_dve))
            per.update(roped=len(lay.roped), r_tmp=len(lay.normed), r_ready=len(lay.normed), normed=len(lay.normed))
            return made, per

        big = {lay.name: layer_sems(lay) for lay in (L1, L2, L3)}
        ffn = {f.name: {k: sem(f"{f.name}_{k}") for k in
                        "g_full g_read d e hm_ready ht_full ht_ready mx_full mx_ready b_full".split()}
               for f in (F0, F1, F2, F3)}
        added_before = {"L0": 0, "F0": 8, "F1": 16, "F2": 24, "F3": 32}

        def done(lay, name, turn, k):
            per = big[lay.name][1][name]
            return turn * per + (per + k)

        def prime(eng, lay, names):
            for k in names.split():
                if k in big[lay.name][0]:
                    eng.sem_inc(big[lay.name][0][k], big[lay.name][1][k])

        def batches(ap):
            return ap.rearrange("p (b r) -> p b r", r=S)

        rope_terms = [[area[:, ROWS + i * HALF:ROWS + (i + 1) * HALF] for i in range(2)] for area in (k_sb, v_sb)]

        def place_of(use):
            if use[0] == "k":
                return batches(k_sb[:, use[2] * HALF:(use[2] + 1) * HALF])
            return qT[:, 8 * use[2]:8 * use[2] + 8, use[3], :]

        def job(what, t):
            return JOBS.index((what, t))

        block = ctx.enter_context(nc.Block())

        @block.sync
        def _(sp):
            for t in range(TILES):
                sp.dma_start(c_nat[:, t, :], a["ctx"][:, t, :]).then_inc(s_ctx[t], 16)
                sp.dma_start(x[:, t, :], a["x"][:, t, :]).then_inc(s_x[t], 16)
                if t == 0:
                    sp.dma_start(w_raw[:, :], a["w"][W_L0Q]).then_inc(w_loaded, 16)
                if t == 1:
                    sp.dma_start(wk_raw, a["wk"]).then_inc(wk_loaded, 16)
            sp.dma_start(kv_raw[:, :], a["kv"][0]).then_inc(kv_loaded, 16)

            def load_w(n, block_):
                sp.wait_ge(w_split, n)
                sp.dma_start(w_raw[:, :], block_).then_inc(w_loaded, 16)

            load_w(W_AG0, a["w"][W_AG0])
            sp.wait_ge(x_added, TILES)
            sp.dma_start(m1_sb[:, :], a["m1"]).then_inc(s_mask, 16)
            sp.dma_start(m2_sb[:, :], a["m2"]).then_inc(s_mask, 16)
            with sp.Fori(W_BASE0, W_F1) as n:
                load_w(n, a["w"][bass.ds(n, 1), :, :].rearrange("a p n -> (a p) n"))
            sp.wait_ge(f1_stored, 32)
            load_w(W_F1, a["f1_store"])
            with sp.Fori(W_F1 + 1, W_BLOCKS) as n:
                load_w(n, a["w"][bass.ds(n - 1, 1), :, :].rearrange("a p n -> (a p) n"))
            for t in range(TILES):
                sp.wait_ge(x_added, added_before["F3"] + t + 1)
                sp.dma_start(out[t], x[:, t, :]).then_inc(s_out, 16)
            sp.wait_ge(s_out, 16 * TILES)

        @block.gpsimd
        def _(pool):
            pool.memset(eps5, 1e-5)
            pool.memset(eps6, 1e-6).then_inc(s_eps, 1)

            def low_w(n, dst):
                pool.wait_ge(w_hi, n + 1)
                for c in range(4):
                    cols = slice(c * 512, (c + 1) * 512)
                    last = nc.gpsimd.tensor_tensor(dst[1][:, cols], w_raw[:, cols], dst[0][:, cols].bitcast(F32), ALU.subtract)
                last.then_inc(w_split, 1)

            def low_kv(n):
                pool.wait_ge(kv_hi, n + 1)
                for c in range(2):
                    cols = slice(c * 512, (c + 1) * 512)
                    last = nc.gpsimd.tensor_tensor(kv_t[1][:, cols], kv_raw[:, cols], kv_t[0][:, cols].bitcast(F32), ALU.subtract)
                last.then_inc(kv_split, 1)

            low_w(W_L0Q, wq_t)
            low_kv(0)
            low_w(W_AG0, wq_t)
            low_w(W_BASE0, wo_t)
            low_w(W_L1Q, wq_t)

            def rope_sums(lay, g, uses):
                own = big[lay.name][0]
                for use in uses:
                    if use not in lay.roped:
                        continue
                    pool.wait_ge(own["ev_dve"], done(lay, "ev_dve", g, lay.by_dve.index(use) + 1))
                    ta, tb = rope_terms[lay.roped.index(use) % 2]
                    nc.gpsimd.tensor_tensor(place_of(use), batches(ta), batches(tb), ALU.add).then_inc(own["roped"], 1)

            for lay in (L1, L2, L3):
                prime(pool, lay, "roped")
                with pool.Fori(0, lay.turns) as g:
                    for sub in range(lay.subs):
                        n = g * (2 * lay.subs) + 2 * sub
                        if lay.rope:
                            rope_sums(lay, g, lay.pre[sub][:5])
                            low_w(n + lay.w_o, wo_t)
                            rope_sums(lay, g, lay.pre[sub][5:] + [u for fill in lay.fill[sub] for u in fill])
                            low_w(n + (lay.w_o + 1), wq_t)
                            low_kv(g + (lay.kv + 1))
                            continue
                        low_w(n + lay.w_o, wo_t)
                        low_w(n + (lay.w_o + 1), wq_t)
                        if sub == lay.subs - 1:
                            low_kv(g + (lay.kv + 1))
                if lay is not L3:
                    low_w(W_L2Q if lay is L1 else W_L3Q, wq_t)
            low_w(W_BASE3, wo_t)

        @block.scalar
        def _(act):
            steps = [0]

            def step(ins):
                steps[0] += 1
                ins.then_inc(act_step, 1)
                act.wait_ge(act_step, steps[0])

            def high_w(n, dst):
                act.wait_ge(w_loaded, n * 16 + 16)
                nc.scalar.activation(dst[0][:, :], w_raw[:, :], ACT.Copy).then_inc(w_hi, 1)

            def high_kv(n):
                act.wait_ge(kv_loaded, n * 16 + 16)
                nc.scalar.activation(kv_t[0][:, :], kv_raw[:, :], ACT.Copy).then_inc(kv_hi, 1)

            def high_turned(what, t, dst):
                n = job(what, t)
                act.wait_ge(tr_full, n + 1)
                nc.scalar.activation(dst, ps[n % 2][:, :].rearrange("p (c r) -> p c r", c=KC), ACT.Copy).then_inc(tr_hi, 1)

            def rows_of(parts_, t):
                return parts_[0][:, :, t * P:(t + 1) * P]

            def norm_x(phase, t):
                n = LN_ORDER.index((phase, t)) + 1
                act.wait_ge(ln_var, n)
                nc.scalar.activation(rstd[:, t:t + 1], mv[:, t, 1:2], ACT.Ln, bias=eps5).then_inc(ln_tmp, 1)
                act.wait_ge(ln_tmp, n)
                nc.scalar.activation(rstd[:, t:t + 1], rstd[:, t:t + 1], ACT.Exp, scale=-0.5).then_inc(ln_rstd, 1)

            nc.scalar.preload_act_table_set("natural_log_exp_and_others")
            act.dma_start(cst[:, :], a["cst"]).then_inc(s_const, 16)
            act.dma_start(qk_raw, a["qkw"]).then_inc(s_const, 16)
            for row, name in ((bq_row, "bq"), (bk_row, "bk"), (fn_row, "fn")):
                act.dma_start(row, a[name].partition_broadcast(P)).then_inc(s_const, 16)

            def l0_feature_norm(t):
                act.wait_ge(s_ctx[t], 16)
                nc.scalar.activation(ctx_squares, c_nat[:, t, :], ACT.Square, accum_out=feat_ss[:, t:t + 1]).then_inc(z["ss_c"], 1)
                act.wait_ge(z["ss_c"], t + 1)
                step(nc.scalar.activation(feat_r[:, t:t + 1], feat_ss[:, t:t + 1], ACT.Ln, scale=1.0 / D, bias=eps6))
                nc.scalar.activation(feat_r[:, t:t + 1], feat_r[:, t:t + 1], ACT.Exp, scale=-0.5).then_inc(z["r_c"], 1)

            act.wait_ge(s_eps, 1)
            l0_feature_norm(0)
            high_turned("ctx", 0, rows_of(cT, 0))
            norm_x(0, 0)
            high_turned(0, 0, rows_of(xT, 0))
            high_turned("feat", 0, oT[0][:, 0, :, :])
            l0_feature_norm(1)
            norm_x(0, 1)
            high_w(W_L0Q, wq_t)
            act.wait_ge(wk_loaded, 16)
            nc.scalar.activation(wo_t[0][:, :], wk_raw, ACT.Copy).then_inc(wk_hi, 1)

            for i in range(TILES + 4):
                if i + 1 < TILES:
                    high_turned("ctx", i + 1, rows_of(cT, i + 1))
                    high_turned(0, i + 1, rows_of(xT, i + 1))
                if i + 2 < TILES:
                    l0_feature_norm(i + 2)
                if 0 <= i - 2 < TILES:
                    t = i - 2
                    act.wait_ge(z["s_read"], 3 * (t + 1))
                    nc.scalar.activation(s_sb[:, (t % 2) * 512:(t % 2) * 512 + P], s_sb[:, (t % 2) * 512:(t % 2) * 512 + P],
                                         ACT.Exp, accum_out=sm[:, t % 2, 0:1]).then_inc(z["exp"], 1)
                if i < TILES:
                    for j in range(2):
                        act.wait_ge(z["qb"], 2 * i + j + 1)
                        nc.scalar.activation(qk_squares[:, j, :], qk_rows[:, i % 2, j, :], ACT.Square,
                                             accum_out=ss0[:, i % 2, j:j + 1]).then_inc(z["ss"], 1)
                    act.wait_ge(z["ss"], 2 * i + 2)
                    step(nc.scalar.activation(r0[:, i % 2, :], ss0[:, i % 2, :], ACT.Ln, scale=1.0 / D, bias=eps6))
                    nc.scalar.activation(r0[:, i % 2, :], r0[:, i % 2, :], ACT.Exp, scale=-0.5).then_inc(z["r"], 1)
                if i + 2 < TILES:
                    norm_x(0, i + 2)
                if 0 <= i - 3 < TILES:
                    norm_x(1, i - 3)
                if 0 <= i - 1 < TILES:
                    t = i - 1
                    act.wait_ge(z["qkt_full"], t + 1)
                    if t >= 1:
                        act.wait_ge(z["s_full"], t)
                    nc.scalar.activation(QT0, ps[4][:, :].rearrange("p (c r) -> p c r", c=KC), ACT.Copy).then_inc(z["qkt_q"], 1)
                if 0 <= i - 2 < TILES:
                    t = i - 2
                    act.wait_ge(z["pt_full"], t + 1)
                    if t >= 2:
                        act.wait_ge(z["av_full"], t - 1)
                    nc.scalar.activation(pt_sb[:, (t % 2) * 512:(t % 2) * 512 + P], ps[6][:, P:2 * P], ACT.Copy).then_inc(z["pt_ready"], 1)
                if i + 1 < TILES:
                    high_turned("feat", i + 1, oT[0][:, (i + 1) % 4, :, :])
                if i == 2:
                    high_kv(0)
                if i == TILES:
                    act.wait_ge(z["qk_full"], 2 * TILES)
                    high_w(W_AG0, wq_t)

            def ffn_act(f, phase):
                fs = ffn[f.name]
                for i in range(TILES + f.next_lag + 1):
                    if 0 <= i - f.next_lag - 1 < TILES and f is not F3:
                        high_turned(phase + 1, i - f.next_lag - 1, rows_of(xT, i - f.next_lag - 1))
                    if i < TILES:
                        high_turned(phase, i, rows_of(xT, i))
                    if 0 <= i - f.add_lag < TILES and f is not F3:
                        norm_x(phase + 1, i - f.add_lag)
                    if 0 <= i - 1 < TILES and f.experts:
                        act.wait_ge(fs["d"], i)
                        if f.mix:
                            nc.scalar.activation(g1[:, 0:f.experts], g1[:, 0:f.experts], ACT.Exp, accum_out=gate_a).then_inc(fs["e"], 1)
                        else:
                            nc.scalar.activation(gate_e, gate_d, ACT.Exp).then_inc(fs["e"], 1)
                    if 0 <= i - 2 < TILES and f.experts:
                        t = i - 2
                        act.wait_ge(fs["ht_full"], t + 1)
                        if t >= 4:
                            act.wait_ge(fs["b_full"], t - 3)
                        src = ps[6][0:f.chunk, 0:f.chunks * P].rearrange("p (c r) -> p c r", c=f.chunks)
                        nc.scalar.activation(hT[0:f.chunk, t % 4, 0:f.chunks, :], src, ACT.Copy).then_inc(fs["ht_ready"], 1)
                    if 0 <= i - 3 < TILES and f.mix:
                        t = i - 3
                        act.wait_ge(fs["mx_full"], t + 1)
                        if t >= 2:
                            act.wait_ge(fs["b_full"], t - 1)
                        nc.scalar.activation(mT[0:16, t % 2, :], ps[7][0:16, 0:P], ACT.Copy, scale=f.scale).then_inc(fs["mx_ready"], 1)
                    if f is F0 and i == 1:
                        high_w(W_BASE0, wo_t)
                    if f is F0 and i in (8, 11):
                        part = (i - 8) // 3
                        act.wait_ge(f1_ready, part + 1)
                        store = a["f1_store"].rearrange("p (c s n) -> p c s n", c=2, s=2)[:, :, part, :]
                        act.dma_start(store, nibf[part].rearrange("p (c n) -> p c n", c=2)).then_inc(f1_stored, 16)
                    if i == TILES and f in (F0, F2):
                        act.wait_ge(fs["g_full"], TILES)
                        high_w(W_L1Q if f is F0 else W_L3Q, wq_t)

            def load_extra(f, n):
                if f.experts:
                    src = a[f"up{f.name}"]
                    act.dma_start(up_w[0:src.shape[0], 0:src.shape[1], :], src).then_inc(extra_loaded, 16)
                if f.mix:
                    act.dma_start(cores, a["cores"]).then_inc(extra_loaded, 16)
                if f.bias:
                    act.dma_start(bias_row, a[f"bias{f.name}"].partition_broadcast(P)).then_inc(extra_loaded, 16)

            act.wait_ge(x_added, TILES)
            load_extra(F0, 0)
            act.dma_start(packed, a["packed"]).then_inc(f1_loaded, 16)
            act.dma_start(scale16, a["scale16"]).then_inc(f1_loaded, 16)
            act.dma_start(mask_words, a["mask8"]).then_inc(f1_loaded, 16)
            ffn_act(F0, 1)
            act.wait_ge(x_added, 2 * TILES)
            act.wait_ge(f1_stored, 32)

            def attend(lay, phase):
                own, per = big[lay.name]
                prime(act, lay, "ev_act exp pt_ready o_hi r_tmp r_ready")
                scale = 1.0 if not lay.wide else float(HD) ** -0.5

                def turn(g, last):
                    def wait(name, k):
                        act.wait_ge(own[name], done(lay, name, g, k))

                    def full(use):
                        wait("full", lay.uses.index(use) + 1)

                    def empty(use):
                        if lay.emptier(use) != "act":
                            return
                        full(use)
                        bank = ps[lay.bank_of[lay.uses.index(use)]]
                        kind = use[0]
                        if kind in "kv":
                            src, half = (use[1], use[2]) if lay.wide else (0, use[2])
                            if lay.wide:
                                inp = bank[:, :].rearrange("p (b r) -> p b r", r=S)
                                area = (k_sb if kind == "k" else vT_sb)[:, :].rearrange("p (b r) -> p b r", r=2 * S)
                                first = 8 * half if kind == "k" else 0
                                dst = area[:, first:first + 8, src * S:(src + 1) * S]
                                if kind == "v" and half == 1:
                                    full(("vt", 0, 1))
                            else:
                                inp, dst = bank[:, :], (k_sb if kind == "k" else vT_sb)[:, half * HALF:(half + 1) * HALF]
                        elif kind == "vt":
                            at = (2 * use[1] + use[2]) if lay.wide else use[1]
                            inp, dst = bank[:, :], v_sb[:, at * 512:(at + 1) * 512]
                        elif kind == "q":
                            inp, dst = bank[:, :].rearrange("p (b r) -> p b r", r=S), qT[:, 8 * use[2]:8 * use[2] + 8, use[3], :]
                        else:
                            m = lay.normed.index(use)
                            r = m1_sb[:, (m % 2) * 512:(m % 2) * 512 + 512]
                            wait("normed", m - 1)
                            nc.scalar.activation(r, bank[:, :], ACT.Ln, scale=1.0 / HD, bias=eps5).then_inc(own["ev_act"], 1)
                            wait("ev_act", lay.by_act.index(use) + 1)
                            nc.scalar.activation(r, r, ACT.Exp, scale=-0.5).then_inc(own["r_ready"], 1)
                            return
                        ins = nc.scalar.activation(dst, inp, ACT.Copy)
                        if lay.norm and kind in "kq":
                            m = lay.normed.index(("ss",) + use)
                            before = lay.normed[m - 2]
                            wait("full", lay.uses.index(before) + 1 - (lay.n if m < 2 else 0))
                            ins = nc.scalar.activation(tmp_sb[:, (m % 2) * 512:(m % 2) * 512 + 512], bank[:, :], ACT.Square)
                        ins.then_inc(own["ev_act"], 1)

                    for sub in range(lay.subs):
                        n = g * (2 * lay.subs) + 2 * sub
                        for use in lay.pre[sub]:
                            if use == ("vt", 0, 0) or (sub and use == lay.pre[sub][0]):
                                if sub:
                                    full(("wo", sub - 1, TILES - 1))
                                else:
                                    wait("full", 0)
                                high_w(n + lay.w_o, wo_t)
                            empty(use)
                        for i in range(len(lay.fill[sub])):
                            if 1 <= i:
                                for use in lay.fill[sub][i - 1]:
                                    empty(use)
                            if 0 <= i - 1 < TILES:
                                t = sub * TILES + i - 1
                                wait("t_full", t + 1)
                                wait("o_full", t - 1)
                                w = 4 * lay.keys
                                nc.scalar.activation(pt_sb[:, (t % 2) * 512:(t % 2) * 512 + w], ps[5][:, 0:w], ACT.Copy)\
                                    .then_inc(own["pt_ready"], 1)
                            if i < TILES:
                                t = sub * TILES + i
                                wait("s_shift", t + 1)
                                w = 4 * lay.keys
                                sv = s_sb[:, (t % 2) * 512:(t % 2) * 512 + w]
                                nc.scalar.activation(sv, sv, ACT.Exp, scale=scale).then_inc(own["exp"], 1)
                            if 0 <= i - 2 < TILES:
                                t = sub * TILES + i - 2
                                wait("o_full", t + 1)
                                if i - 2 >= 4:
                                    full(("wo", sub, i - 6))
                                elif sub:
                                    full(("wo", sub - 1, i + 2))
                                else:
                                    wait("full", lay.uses.index(("wo", lay.subs - 1, i + 2)) + 1 - lay.n)
                                for b in range(2):
                                    ins = nc.scalar.activation(oT[0][:, t % 4, :, b * S:(b + 1) * S],
                                                               ps[6 + b][:, 0:GH * S].rearrange("p (h r) -> p h r", h=GH), ACT.Copy)
                                ins.then_inc(own["o_hi"], 1)
                            if i == 0 and sub == 0:
                                kv_next(g + (lay.kv + 1))
                            if i == 6 and sub == lay.subs - 1:
                                high_kv(g + (lay.kv + 1))
                            if i == 4:
                                full(("q", sub, 1, GH - 1))
                                high_w(n + (lay.w_o + 1), wq_t)
                            if last and sub == lay.subs - 1 and 0 <= i - 5:
                                norm_x(phase + 1, i - 5)

                with act.Fori(0, lay.turns - 1) as g:
                    turn(g, False)
                turn(lay.turns - 1, True)
                for t in range(len(lay.fill[0]) - 5, TILES):
                    norm_x(phase + 1, t)

            def kv_next(n):
                act.wait_ge(kv_split, n)
                act.dma_start(kv_raw[:, :], a["kv"][bass.ds(n, 1), :, :].rearrange("a p n -> (a p) n")).then_inc(kv_loaded, 16)

            attend(L1, 2)

            act.wait_ge(big["L1"][0]["ev_dve"], done(L1, "ev_dve", L1.turns - 1, len(L1.by_dve)))
            load_extra(F1, 0)
            ffn_act(F1, 3)
            act.wait_ge(x_added, 3 * TILES)
            high_w(W_L2Q, wq_t)
            attend(L2, 4)
            act.wait_ge(big["L2"][0]["ev_dve"], done(L2, "ev_dve", L2.turns - 1, len(L2.by_dve)))
            load_extra(F2, 0)
            ffn_act(F2, 5)
            act.wait_ge(x_added, 4 * TILES)
            attend(L3, 6)
            act.wait_ge(big["L3"][0]["ev_dve"], done(L3, "ev_dve", L3.turns - 1, len(L3.by_dve)))
            load_extra(F3, 0)
            high_w(W_BASE3, wo_t)
            ffn_act(F3, 7)

        @block.vector
        def _(dve):
            steps = [0]

            def step(ins):
                steps[0] += 1
                ins.then_inc(dve_step, 1)
                return ins

            def settle():
                dve.wait_ge(dve_step, steps[0])

            def low_turned(what, t, dst):
                n = job(what, t)
                dve.wait_ge(tr_hi, n + 1)
                nc.vector.tensor_tensor(dst[1], ps[n % 2][:, :].rearrange("p (c r) -> p c r", c=KC), dst[0].bitcast(F32),
                                        ALU.subtract).then_inc(tr_lo, 1)

            def rows_of(parts_, t):
                return [p[:, :, t * P:(t + 1) * P] for p in parts_]

            def mean_var(t):
                step(nc.vector.bn_stats(stats[:, 6 * t:6 * t + 6], x[:, t, :]))
                settle()
                nc.vector.bn_aggr(mv[:, t, :], stats[:, 6 * t:6 * t + 6]).then_inc(ln_var, 1)

            def norm_x(phase, t):
                n = XN_ORDER.index((phase, t))
                dve.wait_ge(ln_rstd, LN_ORDER.index((phase, t)) + 1)
                if n >= 2:
                    dve.wait_ge(tr_full, job(*XN_ORDER[n - 2]) + 1)
                nc.vector.tensor_scalar(xn[:, n % 2, :], x[:, t, :], mv[:, t, 0:1], rstd[:, t:t + 1],
                                        ALU.subtract, ALU.mult).then_inc(xn_ready, 1)

            def l0_feature(t):
                dve.wait_ge(z["r_c"], t + 1)
                dve.wait_ge(tr_full, job("ctx", t) + 1)
                nc.vector.scalar_tensor_tensor(out=c_nat[:, t, :], in0=c_nat[:, t, :], scalar=feat_r[:, t:t + 1], in1=fn_row,
                                               op0=ALU.mult, op1=ALU.mult).then_inc(z["feat"], 1)

            def l0_mean_var(t):
                dve.wait_ge(s_x[t], 16)
                mean_var(t)

            l0_mean_var(0)
            norm_x(0, 0)
            dve.wait_ge(s_const, 5 * 16)
            low_turned("ctx", 0, rows_of(cT, 0))
            l0_feature(0)
            low_turned(0, 0, rows_of(xT, 0))
            low_turned("feat", 0, [o[:, 0, :, :] for o in oT])
            l0_mean_var(1)
            norm_x(0, 1)
            step(nc.vector.tensor_tensor(qk_w[:, 0:4], qk_raw[:, 0:4], qk_raw[:, 4:8], ALU.mult))
            step(nc.vector.tensor_tensor(qk_w[:, 4:5], qk_raw[:, 8:9], qk_raw[:, 9:10], ALU.mult))
            dve.wait_ge(wk_hi, 1)
            nc.vector.tensor_tensor(wo_t[1][:, :], wk_raw, wo_t[0][:, :].bitcast(F32), ALU.subtract).then_inc(wk_split, 1)
            dve.wait_ge(wk_split, 1)
            for i in range(TILES + 4):
                if i + 1 < TILES:
                    low_turned("ctx", i + 1, rows_of(cT, i + 1))
                    l0_feature(i + 1)
                    low_turned(0, i + 1, rows_of(xT, i + 1))
                if 0 <= i - 2 < TILES:
                    t = i - 2
                    sv = s_sb[:, (t % 2) * 512:(t % 2) * 512 + P]
                    dve.wait_ge(z["s_full"], t + 1)
                    if t >= 2:
                        dve.wait_ge(z["pt_full"], t - 1)
                    nc.vector.scalar_tensor_tensor(out=sv, in0=ps[6][:, 0:P], scalar=float(D) ** -0.5, in1=blk,
                                                   op0=ALU.mult, op1=ALU.add).then_inc(z["s_read"], 1)
                    dve.wait_ge(z["s_read"], 3 * t + 1)
                    nc.vector.tensor_reduce(mx[:, t % 2, 0:1], sv, AX_X, ALU.max).then_inc(z["s_read"], 1)
                    dve.wait_ge(z["s_read"], 3 * t + 2)
                    nc.vector.tensor_scalar(sv, sv, mx[:, t % 2, 0:1], None, ALU.subtract).then_inc(z["s_read"], 1)
                if 0 <= i - 2 < TILES:
                    dve.wait_ge(z["exp"], t + 1)
                    step(nc.vector.reciprocal(rc[:, t % 2, 0:1], sm[:, t % 2, 0:1]))
                    settle()
                    nc.vector.tensor_scalar(sv, sv, rc[:, t % 2, 0:1], None, ALU.mult).then_inc(z["p_ready"], 1)
                if i < TILES:
                    for j in range(2):
                        dve.wait_ge(z["qk_full"], 2 * i + j + 1)
                        if i >= 2:
                            dve.wait_ge(z["qkt_full"], i - 1)
                        nc.vector.tensor_tensor(qk_rows[:, i % 2, j, :], ps[2 + j][:, :], (bq_row, bk_row)[j], ALU.add)\
                            .then_inc(z["qb"], 1)
                if i + 2 < TILES:
                    l0_mean_var(i + 2)
                if 0 <= i - 3 < TILES:
                    t = i - 3
                    dve.wait_ge(z["av_full"], t + 1)
                    nc.vector.tensor_tensor(x[:, t, :], ps[7][:, :], x[:, t, :], ALU.add).then_inc(x_added, 1)
                    dve.wait_ge(x_added, t + 1)
                    mean_var(t)
                if i < TILES:
                    dve.wait_ge(z["r"], i + 1)
                    for j in range(2):
                        nc.vector.tensor_scalar(qk_rows[:, i % 2, j, :], qk_rows[:, i % 2, j, :], r0[:, i % 2, j:j + 1], None,
                                                ALU.mult).then_inc(z["qn"], 1)
                if i + 2 < TILES:
                    norm_x(0, i + 2)
                if TILES <= i < TILES + 2:
                    norm_x(1, i - TILES)
                if 0 <= i - 1 < TILES:
                    t = i - 1
                    dve.wait_ge(z["qkt_full"], t + 1)
                    if t >= 1:
                        dve.wait_ge(z["s_full"], t)
                    nc.vector.tensor_tensor(KT0, ps[5][:, :].rearrange("p (c r) -> p c r", c=KC),
                                            qk_w[:, 0:4].unsqueeze(2).to_broadcast([P, KC, P]), ALU.mult).then_inc(z["qkt_k"], 1)
                if i + 1 < TILES:
                    low_turned("feat", i + 1, [o[:, (i + 1) % 4, :, :] for o in oT])

            def gates_top2(f, t, fs, bank):
                e, w = f.experts, f.wide
                step(nc.vector.tensor_copy(lg[:, 0:e], bank[:, w:w + e]))
                settle()
                step(nc.vector.max(top8, lg[:, 0:max(e, 8)]))
                settle()
                step(nc.vector.max_index(idx8[:, :], top8, lg[:, 0:max(e, 8)]))
                nc.vector.tensor_tensor(gate_d, top8[:, 1:2], top8[:, 0:1], ALU.subtract).then_inc(fs["d"], 1)
                settle()
                step(nc.vector.tensor_copy(idxf, idx8[:, 0:2]))
                dve.wait_ge(fs["e"], t + 1)
                step(nc.vector.tensor_scalar(gate_a, gate_e, 1.0, None, ALU.add))
                settle()
                step(nc.vector.reciprocal(gate_r, gate_a))
                settle()
                step(nc.vector.tensor_scalar(gate_p, gate_r, f.scale, None, ALU.mult))
                settle()
                step(nc.vector.tensor_tensor(gate_p2, gate_p, gate_e, ALU.mult))
                step(nc.vector.tensor_scalar(g1[:, 0:e], iota[:, 0:e], idxf[:, 0:1], gate_p, ALU.is_equal, ALU.mult))
                settle()
                step(nc.vector.tensor_scalar(lg[:, 0:e], iota[:, 0:e], idxf[:, 1:2], gate_p2, ALU.is_equal, ALU.mult))
                settle()
                step(nc.vector.tensor_tensor(g1[:, 0:e], g1[:, 0:e], lg[:, 0:e], ALU.add))
                settle()
                nc.vector.tensor_tensor(hm[:, t % 2, 0:w].rearrange("p (e r) -> p e r", e=e),
                                        bank[:, 0:w].rearrange("p (e r) -> p e r", e=e),
                                        g1[:, 0:e].unsqueeze(2).to_broadcast([P, e, f.rank]), ALU.mult).then_inc(fs["hm_ready"], 1)

            def gates_all(f, t, fs, bank):
                e, r = f.experts, f.rank
                step(nc.vector.tensor_reduce(gate_d, bank[:, r:r + e], AX_X, ALU.max))
                settle()
                nc.vector.tensor_scalar(g1[:, 0:e], bank[:, r:r + e], gate_d, None, ALU.subtract).then_inc(fs["d"], 1)
                step(nc.vector.tensor_copy(lg[:, 0:r], bank[:, 0:r]))
                dve.wait_ge(fs["e"], t + 1)
                step(nc.vector.reciprocal(gate_r, gate_a))
                settle()
                step(nc.vector.tensor_scalar(g1[:, 0:e], g1[:, 0:e], gate_r, None, ALU.mult))
                settle()
                nc.vector.tensor_tensor(hm[:, t % 2, 0:e * r].rearrange("p (e r) -> p e r", e=e),
                                        lg[:, 0:r].unsqueeze(1).to_broadcast([P, e, r]),
                                        g1[:, 0:e].unsqueeze(2).to_broadcast([P, e, r]), ALU.mult).then_inc(fs["hm_ready"], 1)

            def f1_weight(i):
                part = (i - 1) // 3
                if i == 0:
                    dve.wait_ge(f1_loaded, 3 * 16)
                    step(nc.vector.tensor_scalar(nibf[0], mask8, 0.5, 0.5, ALU.mult, ALU.add))
                    settle()
                    step(nc.vector.tensor_tensor(sc_f, scale16, nibf[0], ALU.mult))
                elif i % 3 == 1:
                    if part:
                        step(nc.vector.tensor_scalar(nib, packed, 4, 15, ALU.logical_shift_right, ALU.bitwise_and))
                    else:
                        step(nc.vector.tensor_scalar(nib, packed, 15, None, ALU.bitwise_and))
                elif i % 3 == 2:
                    settle()
                    step(nc.vector.tensor_copy(nibf[part], nib))
                else:
                    settle()
                    nc.vector.scalar_tensor_tensor(out=nibf[part], in0=nibf[part], scalar=-8.0, in1=sc_f, op0=ALU.add, op1=ALU.mult)\
                        .then_inc(f1_ready, 1)

            def ffn_dve(f, phase, extra):
                fs = ffn[f.name]
                if 0 < f.experts < 8 and not f.mix:
                    step(nc.vector.memset(lg[:, f.experts:8], -3.0e38))
                for i in range(TILES + f.next_lag + 1):
                    if 0 <= i - f.next_lag - 1 < TILES and f is not F3:
                        t = i - f.next_lag - 1
                        low_turned(phase + 1, t, rows_of(xT, t))
                    if 2 <= i + 1 < TILES:
                        norm_x(phase, i + 1)
                    if i < TILES:
                        low_turned(phase, i, rows_of(xT, i))
                    if 0 <= i - f.add_lag < TILES:
                        t = i - f.add_lag
                        if f.bias:
                            dve.wait_ge(extra_loaded, extra)
                            step(nc.vector.tensor_tensor(x[:, t, :], x[:, t, :], bias_row, ALU.add))
                            settle()
                        dve.wait_ge(fs["b_full"], t + 1)
                        nc.vector.tensor_tensor(x[:, t, :], ps[4 + t % 2][:, :], x[:, t, :], ALU.add).then_inc(x_added, 1)
                        if f is not F3:
                            dve.wait_ge(x_added, added_before[f.name] + t + 1)
                            mean_var(t)
                    if 0 <= i - 1 < TILES and f.experts:
                        t = i - 1
                        dve.wait_ge(fs["g_full"], t + 1)
                        if t >= 2:
                            dve.wait_ge(fs["ht_full"], t - 1)
                        (gates_all if f.mix else gates_top2)(f, t, fs, ps[2 + t % 2])
                    if f is F0 and 2 <= i < 9:
                        f1_weight(i - 2)
                    if 0 <= i - f.add_lag < TILES and f is not F3:
                        norm_x(phase + 1, i - f.add_lag)

            def attend(lay, phase):
                own, per = big[lay.name]
                prime(dve, lay, "ev_dve s_read s_max s_shift s_sum s_rec p_ready o_lo normed")
                if lay is L1:
                    dve.wait_ge(s_mask, 32)
                    dve.wait_ge(f1_stored, 32)

                def turn(g, last):
                    def wait(name, k):
                        dve.wait_ge(own[name], done(lay, name, g, k))

                    def full(use):
                        wait("full", lay.uses.index(use) + 1)

                    def table(c, rows):
                        return cst[rows, c:c + S].unsqueeze(1).to_broadcast([rows.stop - rows.start, HALF // S, S])

                    def rope(bank, use):
                        m = lay.roped.index(use)
                        wait("roped", m - 1)
                        ta, tb = rope_terms[m % 2]
                        nc.vector.tensor_tensor(batches(ta), batches(bank[:, :]), table(C_COS, slice(0, P)), ALU.mult)
                        for lo, hi in ((0, 64), (64, 0)):
                            ins = nc.vector.tensor_tensor(batches(tb[lo:lo + 64, :]), batches(bank[hi:hi + 64, :]),
                                                          table(C_SIN, slice(hi, hi + 64)), ALU.mult)
                        ins.then_inc(own["ev_dve"], 1)

                    def empty(use):
                        kind = use[0]
                        if kind == "ss":
                            m = lay.normed.index(use)
                            wait("r_ready", m + 1)
                            r = m1_sb[:, (m % 2) * 512:(m % 2) * 512 + 512]
                            if use[1] == "k":
                                kk = k_sb[:, use[3] * HALF:(use[3] + 1) * HALF]
                                ins = nc.vector.scalar_tensor_tensor(out=kk, in0=kk, scalar=qk_w[:, 4:5], in1=r, op0=ALU.mult, op1=ALU.mult)
                            else:
                                qq = qT[:, 8 * use[3]:8 * use[3] + 8, use[4], :]
                                ins = nc.vector.tensor_tensor(qq, qq, batches(r), ALU.mult)
                            ins.then_inc(own["normed"], 1)
                            return
                        if lay.emptier(use) != "dve":
                            return
                        full(use)
                        bank = ps[lay.bank_of[lay.uses.index(use)]]
                        if kind in "kq":
                            rope(bank, use)
                        else:
                            t = use[2]
                            if use[1]:
                                wait("ev_dve", lay.by_dve.index(("wo", use[1] - 1, t)) + 1)
                            else:
                                wait("ev_dve", lay.by_dve.index(("wo", lay.subs - 1, t)) + 1 - len(lay.by_dve))
                            nc.vector.tensor_tensor(x[:, t, :], bank[:, :], x[:, t, :], ALU.add).then_inc(own["ev_dve"], 1)

                    for sub in range(lay.subs):
                        for use in lay.pre[sub]:
                            empty(use)
                        for i in range(len(lay.fill[sub]) + 1):
                            t = sub * TILES + i
                            w = lay.keys
                            sv = s_sb[:, (t % 2) * 512:(t % 2) * 512 + 4 * w].rearrange("p (j k) -> p j k", j=4)
                            before_scores = [u for u in lay.fill[sub][i - 1] if u[0] == "ss"] if i >= 1 else []
                            for use in before_scores:
                                empty(use)
                            if i < TILES:
                                scores = ps[3 + t % 2][:, :].rearrange("p (j k) -> p j k", j=4)[:, :, 0:w]
                                wait("s_full", t + 1)
                                wait("t_full", t - 1)
                                if lay.wide:
                                    src = scores
                                else:
                                    pair = lambda ap: ap.rearrange("p (h b) k -> p h b k", h=2)
                                    if lay.rope:
                                        m = m1_sb[:, 2 * i * S:2 * (i + 1) * S].rearrange("p (b k) -> p b k", b=2)
                                        m = m.unsqueeze(1).to_broadcast([P, 2, 2, S])
                                        nc.vector.scalar_tensor_tensor(out=pair(sv), in0=pair(scores), scalar=float(HD) ** -0.5,
                                                                       in1=m, op0=ALU.mult, op1=ALU.add).then_inc(own["s_read"], 1)
                                    else:
                                        m = m2_sb[:, :].unsqueeze(1).to_broadcast([P, 4, S])
                                        nc.vector.scalar_tensor_tensor(out=sv, in0=scores, scalar=float(HD) ** -0.5,
                                                                       in1=m, op0=ALU.mult, op1=ALU.add).then_inc(own["s_read"], 1)
                                    wait("s_read", t + 1)
                                    src = sv
                                nc.vector.tensor_reduce(mx[:, t % 2, :], src, AX_X, ALU.max).then_inc(own["s_max"], 1)
                                wait("s_max", t + 1)
                                ins = nc.vector.tensor_tensor(sv, src, mx[:, t % 2, :].unsqueeze(2).to_broadcast([P, 4, w]), ALU.subtract)
                                ins.then_inc(own["s_shift"], 1)
                            if i >= 1:
                                for use in lay.fill[sub][i - 1]:
                                    if use not in before_scores:
                                        empty(use)
                                    if last and use[0] == "wo" and sub == lay.subs - 1:
                                        wait("ev_dve", lay.by_dve.index(use) + 1)
                                        mean_var(use[2])
                            if i < TILES:
                                wait("exp", t + 1)
                                nc.vector.tensor_reduce(sm[:, t % 2, :], sv, AX_X, ALU.add).then_inc(own["s_sum"], 1)
                                wait("s_sum", t + 1)
                                nc.vector.reciprocal(rc[:, t % 2, :], sm[:, t % 2, :]).then_inc(own["s_rec"], 1)
                                wait("s_rec", t + 1)
                                nc.vector.tensor_tensor(sv, sv, rc[:, t % 2, :].unsqueeze(2).to_broadcast([P, 4, w]), ALU.mult)\
                                    .then_inc(own["p_ready"], 1)
                            if 0 <= i - 2 < TILES:
                                u = t - 2
                                wait("o_hi", u + 1)
                                for b in range(2):
                                    cols = slice(b * S, (b + 1) * S)
                                    ins = nc.vector.tensor_tensor(oT[1][:, u % 4, :, cols],
                                                                  ps[6 + b][:, 0:GH * S].rearrange("p (h r) -> p h r", h=GH),
                                                                  oT[0][:, u % 4, :, cols].bitcast(F32), ALU.subtract)
                                ins.then_inc(own["o_lo"], 1)
                            if last and sub == lay.subs - 1 and i in (9, 10):
                                norm_x(phase + 1, i - 9)

                with dve.Fori(0, lay.turns - 1) as g:
                    turn(g, False)
                turn(lay.turns - 1, True)
                dve.wait_ge(own["ev_dve"], done(lay, "ev_dve", lay.turns - 1, len(lay.by_dve)))

            ffn_dve(F0, 1, 0)
            attend(L1, 2)
            ffn_dve(F1, 3, 16 * (1 + 1))
            attend(L2, 4)
            ffn_dve(F2, 5, 0)
            attend(L3, 6)
            ffn_dve(F3, 7, 16 * (1 + 1 + 1 + 3))

        @block.tensor
        def _(pe):
            def product(dst, lhs, rhs, first, last):
                nc.tensor.matmul(dst, lhs[0], rhs[0], start=first, stop=False)
                nc.tensor.matmul(dst, lhs[0], rhs[1], start=False, stop=False)
                return nc.tensor.matmul(dst, lhs[1], rhs[0], start=False, stop=last)

            def turn(what, t, src, every_second=False):
                n = job(what, t)
                if n >= 2:
                    pe.wait_ge(tr_lo, n - 1)
                for c in range(KC):
                    if every_second:
                        part = src[:, (c // 2) * 256:(c // 2 + 1) * 256].rearrange("p (r s) -> p s r", s=2)[:, c % 2, :]
                    else:
                        part = src[:, c * P:(c + 1) * P]
                    ins = nc.tensor.transpose(ps[n % 2][:, c * P:(c + 1) * P], part, ident)
                ins.then_inc(tr_full, 1)

            def turn_x(phase, t):
                n = XN_ORDER.index((phase, t))
                pe.wait_ge(xn_ready, n + 1)
                turn(phase, t, xn[:, n % 2, :], phase == 3)

            def rows(parts_, c, t):
                return [p[:, c, t * P:(t + 1) * P] for p in parts_]

            def l0_turns(t):
                pe.wait_ge(s_ctx[t], 16)
                turn("ctx", t, c_nat[:, t, :])
                turn_x(0, t)

            def l0_turn_feature(t):
                pe.wait_ge(z["feat"], t + 1)
                turn("feat", t, c_nat[:, t, :])

            pe.wait_ge(s_const, 5 * 16)
            l0_turns(0)
            l0_turn_feature(0)
            for i in range(TILES + 4):
                if i + 1 < TILES:
                    l0_turns(i + 1)
                if i < TILES:
                    pe.wait_ge(tr_lo, job("feat", i) + 1)
                    for j in range(2):
                        pe.wait_ge((w_split, wk_split)[j], 1)
                        if i >= 1:
                            pe.wait_ge(z["qb"], 2 * (i - 1) + j + 1)
                        for c in range(KC):
                            lhs = rows(xT, c, i) if j == 0 else [o[:, i % 4, c, :] for o in oT]
                            w = (wq, wo)[j]
                            ins = product(ps[2 + j][:, :], lhs, [p[:, c, :] for p in w], c == 0, c == KC - 1)
                        ins.then_inc(z["qk_full"], 1)
                if 0 <= i - 1 < TILES:
                    t = i - 1
                    pe.wait_ge(z["qn"], 2 * (t + 1))
                    if t >= 1:
                        pe.wait_ge(z["qkt_q"], t)
                        pe.wait_ge(z["qkt_k"], t)
                    for j in range(2):
                        for c in range(KC):
                            ins = nc.tensor.transpose(ps[4 + j][:, c * P:(c + 1) * P], qk_rows[:, t % 2, j, c * P:(c + 1) * P], ident)
                    ins.then_inc(z["qkt_full"], 1)
                if 0 <= i - 2 < TILES:
                    t = i - 2
                    pe.wait_ge(z["p_ready"], t + 1)
                    nc.tensor.transpose(ps[6][:, P:2 * P], s_sb[:, (t % 2) * 512:(t % 2) * 512 + P], ident).then_inc(z["pt_full"], 1)
                if 0 <= i - 3 < TILES:
                    t = i - 3
                    pe.wait_ge(z["pt_ready"], t + 1)
                    if t >= 1:
                        pe.wait_ge(x_added, t)
                    nc.tensor.matmul(ps[7][:, :], pt_sb[:, (t % 2) * 512:(t % 2) * 512 + P], c_nat[:, t, :], start=True, stop=True)\
                        .then_inc(z["av_full"], 1)
                if 0 <= i - 1 < TILES:
                    t = i - 1
                    pe.wait_ge(z["qkt_q"], t + 1)
                    pe.wait_ge(z["qkt_k"], t + 1)
                    if t >= 1:
                        pe.wait_ge(z["pt_ready"], t)
                    for c in range(KC):
                        ins = nc.tensor.matmul(ps[6][:, 0:P], QT0[:, c, :], KT0[:, c, :], start=(c == 0), stop=(c == KC - 1))
                    ins.then_inc(z["s_full"], 1)
                if i + 1 < TILES:
                    l0_turn_feature(i + 1)

            def ffn_pe(f, phase, w_need, extra, before):
                fs = ffn[f.name]
                base_w = wo if f.experts else wq
                for i in range(TILES + f.next_lag):
                    if i < 2 and before:
                        last = [k for k, u in enumerate(before.uses) if before.bank_of[k] == job(phase, i) % 2][-1]
                        use = before.by_dve.index(before.uses[last])
                        pe.wait_ge(big[before.name][0]["ev_dve"], done(before, "ev_dve", before.turns - 1, use + 1))
                    if i < TILES:
                        turn_x(phase, i)
                    if 0 <= i - 1 < TILES and f.experts:
                        t = i - 1
                        pe.wait_ge(w_split, w_need)
                        pe.wait_ge(tr_lo, job(phase, t) + 1)
                        if t >= 2:
                            pe.wait_ge(fs["hm_ready"], t - 1)
                        for c in range(KC):
                            ins = product(ps[2 + t % 2][:, 0:UPW], rows(xT, c, t), [p[:, c, 0:UPW] for p in wq], c == 0, c == KC - 1)
                        ins.then_inc(fs["g_full"], 1)
                    if 0 <= i - 2 < TILES and f.experts:
                        t = i - 2
                        pe.wait_ge(fs["hm_ready"], t + 1)
                        if t >= 1:
                            pe.wait_ge(fs["ht_ready"], t)
                        for c in range(f.chunks):
                            ins = nc.tensor.transpose(ps[6][0:f.chunk, c * P:(c + 1) * P], hm[:, t % 2, c * f.chunk:(c + 1) * f.chunk], ident)
                        ins.then_inc(fs["ht_full"], 1)
                    if 0 <= i - 3 < TILES and f.mix:
                        t = i - 3
                        pe.wait_ge(extra_loaded, extra)
                        pe.wait_ge(fs["ht_ready"], t + 1)
                        if t >= 1:
                            pe.wait_ge(fs["mx_ready"], t)
                        nc.tensor.matmul(ps[7][0:16, 0:P], cores, hT[:, t % 4, 0, :], start=True, stop=True).then_inc(fs["mx_full"], 1)
                    if 0 <= i - f.out_lag < TILES:
                        t = i - f.out_lag
                        if t >= 2:
                            pe.wait_ge(x_added, added_before[f.name] + t - 1)
                        bank = ps[4 + t % 2][:, :]
                        if f.base:
                            pe.wait_ge(tr_lo, job(phase, t) + 1)
                            pe.wait_ge(w_split, w_need + (1 if f.experts else 0))
                            for c in range(KC):
                                ins = product(bank, rows(xT, c, t), [p[:, c, :] for p in base_w], c == 0, c == KC - 1 and not f.experts)
                        if f.experts:
                            pe.wait_ge(extra_loaded, extra)
                            if f.mix:
                                pe.wait_ge(fs["mx_ready"], t + 1)
                                ins = nc.tensor.matmul(bank, mT[0:16, t % 2, :], up_w[0:16, 0, :], start=False, stop=True)
                            else:
                                pe.wait_ge(fs["ht_ready"], t + 1)
                                for c in range(f.chunks):
                                    ins = nc.tensor.matmul(bank, hT[0:f.chunk, t % 4, c, :], up_w[0:f.chunk, c, :],
                                                           start=(not f.base and c == 0), stop=(c == f.chunks - 1))
                        ins.then_inc(fs["b_full"], 1)
                    if 0 <= i - f.next_lag < TILES and f is not F3:
                        turn_x(phase + 1, i - f.next_lag)

            def attend(lay, phase):
                own, per = big[lay.name]
                prime(pe, lay, "full s_full t_full o_full")
                pe.wait_ge(tr_lo, job(phase, TILES - 1) + 1)
                with pe.Fori(0, lay.turns) as g:
                    def wait(name, k):
                        pe.wait_ge(own[name], done(lay, name, g, k))

                    def emptied(use, turns_ago=0):
                        who = lay.emptier(use)
                        these = lay.by_act if who == "act" else lay.by_dve
                        wait(f"ev_{who}", these.index(use) + 1 - turns_ago * len(these))

                    def usable(use):
                        if lay.rope:
                            wait("roped", lay.roped.index(use) + 1)
                        elif lay.norm:
                            wait("normed", lay.normed.index(("ss",) + use) + 1)
                        else:
                            emptied(use)

                    def dense(use):
                        before, turn_before = lay.before(use)
                        emptied(before, int(turn_before))
                        bank = ps[lay.bank_of[lay.uses.index(use)]]
                        kind = use[0]
                        if kind in "kv":
                            src = xT if lay.wide and use[1] == 1 else cT
                            half = use[2]
                            if use == lay.uses[0]:
                                pe.wait_ge(kv_split, g + (lay.kv + 1))
                            for c in range(KC):
                                ins = product(bank[:, :], [p[:, "kv".index(kind), c, :] for p in wkv],
                                              [p[:, c, half * HALF:(half + 1) * HALF] for p in src], c == 0, c == KC - 1)
                        elif kind == "vt":
                            if lay.wide:
                                emptied(("v", 1, use[1]))
                                first = 4 * use[2]
                            else:
                                emptied(("v", 0, use[1]))
                                first = 4 * use[1]
                            for j in range(4):
                                ins = nc.tensor.transpose(bank[:, j * P:(j + 1) * P], vT_sb[:, (first + j) * P:(first + j + 1) * P], ident)
                        elif kind == "q":
                            _, sub, half, h = use
                            if half == 0 and h == 0:
                                n = g * (2 * lay.subs) + 2 * sub
                                pe.wait_ge(w_split, n + lay.w_o)
                            for c in range(KC):
                                ins = product(bank[:, :], [p[:, c, h * HD:(h + 1) * HD] for p in wq],
                                              [p[:, c, half * HALF:(half + 1) * HALF] for p in xT], c == 0, c == KC - 1)
                        elif kind == "ss":
                            m = lay.normed.index(use)
                            emptied(use[1:])
                            ins = nc.tensor.matmul(bank[:, :], ones, tmp_sb[:, (m % 2) * 512:(m % 2) * 512 + 512], start=True, stop=True)
                        else:
                            _, sub, t = use
                            if t == 0:
                                n = g * (2 * lay.subs) + 2 * sub
                                pe.wait_ge(w_split, n + (lay.w_o + 1))
                            wait("o_lo", sub * TILES + t + 1)
                            for h in range(GH):
                                ins = product(bank[:, :], [o[:, t % 4, h, :] for o in oT], [p[:, h, :] for p in wo], h == 0, h == GH - 1)
                        ins.then_inc(own["full"], 1)

                    for sub in range(lay.subs):
                        for use in lay.pre[sub]:
                            dense(use)
                        for i in range(len(lay.fill[sub])):
                            if i < TILES:
                                t = sub * TILES + i
                                if i == 0:
                                    if sub == 0:
                                        for use in lay.pre[0]:
                                            if use[0] == "k":
                                                last_k = use
                                        usable(last_k)
                                    usable(("q", sub, 0, GH - 1))
                                if i == 4:
                                    usable(("q", sub, 1, GH - 1))
                                wait("s_read" if not lay.wide else "s_shift", t - 1)
                                for hp in range(2):
                                    for b in range(2):
                                        lhs = qT[:, 2 * i + b, 2 * hp:2 * hp + 2, :]
                                        if lay.wide:
                                            off = (2 * hp + b) * P
                                            keys = k_sb[:, (2 * i + b) * 2 * S:(2 * i + b + 1) * 2 * S]
                                        else:
                                            off = 2 * hp * P + b * S
                                            keys = k_sb[:, i * P:(i + 1) * P]
                                        ins = nc.tensor.matmul(ps[3 + t % 2][:, off:off + P], lhs, keys, start=True, stop=True)
                                ins.then_inc(own["s_full"], 1)
                            if 0 <= i - 1 < TILES:
                                t = sub * TILES + i - 1
                                wait("p_ready", t + 1)
                                wait("pt_ready", t)
                                for j in range(4 * lay.keys // P):
                                    ins = nc.tensor.transpose(ps[5][:, j * P:(j + 1) * P],
                                                              s_sb[:, (t % 2) * 512 + j * P:(t % 2) * 512 + (j + 1) * P], ident)
                                ins.then_inc(own["t_full"], 1)
                            if 0 <= i - 2 < TILES:
                                t = sub * TILES + i - 2
                                if i == 2 and sub == 0:
                                    for use in lay.pre[0]:
                                        if use[0] == "vt":
                                            last_v = use
                                    emptied(last_v)
                                wait("pt_ready", t + 1)
                                wait("o_lo", t)
                                for b in range(2):
                                    if lay.wide:
                                        lhs = v_sb[:, (2 * (i - 2) + b) * P:(2 * (i - 2) + b + 1) * P]
                                        rhs = pt_sb[:, (t % 2) * 512:(t % 2 + 1) * 512].rearrange("p (h b r) -> p h b r", h=2, b=2)[:, :, b, :]
                                    else:
                                        lhs = v_sb[b * S:(b + 1) * S, (i - 2) * P:(i - 1) * P]
                                        rhs = pt_sb[b * S:(b + 1) * S, (t % 2) * 512:(t % 2) * 512 + 4 * S]
                                    ins = nc.tensor.matmul(ps[6 + b][:, 0:GH * S], lhs, rhs, start=True, stop=True)
                                ins.then_inc(own["o_full"], 1)
                            for use in lay.fill[sub][i]:
                                dense(use)

            ffn_pe(F0, 1, W_AG0 + 1, 16, None)
            attend(L1, 2)
            ffn_pe(F1, 3, W_F1 + 1, 0, L1)
            attend(L2, 4)
            ffn_pe(F2, 5, W_AG2 + 1, 16 * (1 + 1 + 1), L2)
            attend(L3, 6)
            ffn_pe(F3, 7, W_AG3 + 1, 16 * (1 + 1 + 1 + 3), L3)


def kernel(**inputs):
    import concourse.bacc as bacc
    from concourse.bass_utils import run_bass_kernel_spmd

    f = {k: np.asarray(v) for k, v in inputs.items()}

    def tiles(m):
        return np.ascontiguousarray(m.reshape(TILES, P, D).transpose(1, 0, 2))

    def by_input(m):
        wide = np.zeros((D, D), m.dtype)
        wide[:, :m.shape[1]] = m
        return wide.reshape(KC, P, D).transpose(1, 0, 2).reshape(P, KC * D)

    def by_head(m):
        return m.reshape(GH, HD, D).transpose(1, 0, 2).reshape(P, GH * D)

    span = GH * HD
    qs = {1: f["L1_xattn_wq"], 2: f["L2_xattn_Wq"].T, 3: f["L3_xattn_Wq"]}
    os_ = {1: f["L1_xattn_wo"], 2: f["L2_xattn_Wo"].T, 3: f["L3_xattn_Wo"]}
    down0 = np.concatenate([f["L0_ffn_lora_A"].reshape(-1, D), f["L0_ffn_gate_W"]]).T
    down2 = np.concatenate([f["L2_ffn_A"].reshape(-1, D), f["L2_ffn_router_w"]]).T
    down3 = np.concatenate([f["L3_ffn_A_w"], f["L3_ffn_router_w"]]).T
    w = [by_input(f["L0_xattn_Wq_w"].T), by_input(down0), by_input(f["L0_ffn_base_W"].T)]
    for lay in (1, 2, 3):
        w.append(by_input(qs[lay][:, :span]))
        for n in range(GROUPS):
            w.append(by_head(os_[lay][n * span:(n + 1) * span]))
            if n + 1 < GROUPS:
                w.append(by_input(qs[lay][:, (n + 1) * span:(n + 2) * span]))
        if lay > 1:
            w.append(by_input(down2 if lay == 2 else down3))
    w.append(by_input(f["L3_ffn_W_base"].T))
    assert len(w) == W_BLOCKS - 1
    kv = []
    for k_w, v_w, heads in ((f["L1_xattn_wk"], f["L1_xattn_wv"], 8), (f["L2_xattn_Wk"].T, f["L2_xattn_Wv"].T, 8),
                            (f["L3_xattn_Wk"], f["L3_xattn_Wv"], 4)):
        for h in range(heads):
            pair = np.stack([m[:, h * HD:(h + 1) * HD].reshape(KC, P, HD) for m in (k_w, v_w)])
            kv.append(pair.transpose(2, 0, 1, 3).reshape(P, 2 * KC * HD))
    kv.append(kv[-1])

    cst = np.zeros((P, C_END), np.float32)
    cst[:, C_ID:C_ID + P] = np.eye(P)
    cst[:, C_ONE:C_ONE + P] = 1.0
    cst[:, C_BLK:C_BLK + P] = np.where(np.arange(P)[:, None] // S == np.arange(P)[None, :] // S, 0.0, NEG)
    inv = (1.0 / np.float32(10000.0) ** (np.arange(0, HD, 2, dtype=np.float32) / np.float32(HD))).astype(np.float32)
    ang = (np.arange(S, dtype=np.float32)[None, :] * inv[:, None]).astype(np.float32)
    cst[:, C_COS:C_COS + S] = np.concatenate([np.cos(ang), np.cos(ang)])
    cst[:, C_SIN:C_SIN + S] = np.concatenate([np.sin(ang), -np.sin(ang)])
    cst[:, C_IOTA:C_IOTA + 32] = np.arange(32)

    columns = [f["L0_xattn_qn_w"].reshape(KC, P).T, f["L0_xattn_kn_w"].reshape(KC, P).T,
               f["L2_xattn_q_norm_w"][:, None], f["L2_xattn_k_norm_w"][:, None]]
    m1 = f["mask_BxSxS2_ff0"].transpose(1, 0, 2).reshape(S, B * S)
    m2 = f["mask_1x1xSxS2_ff0"].reshape(S, S)
    blocks = D // 32
    packed = f["L1_ffn_weight_packed"].reshape(D, blocks * 16).T.reshape(2, P, D)
    over = lambda v: np.repeat(v.reshape(D, blocks).T, 16, axis=0).reshape(2, P, D).transpose(1, 0, 2).reshape(P, 2 * D)
    arrays = {
        "x": tiles(f["x"].reshape(ROWS, D)),
        "ctx": tiles(f["ctx_4096"].reshape(ROWS, D)),
        "w": np.stack(w),
        "kv": np.stack(kv),
        "wk": by_input(f["L0_xattn_Wk_w"].T),
        "cst": cst,
        "qkw": np.concatenate(columns, axis=1),
        "bq": f["L0_xattn_Wq_b"],
        "bk": f["L0_xattn_Wk_b"],
        "fn": f["L0_xattn_fn_w"],
        "m1": np.concatenate([m1, m1]),
        "m2": np.concatenate([m2, m2]),
        "packed": packed.transpose(1, 0, 2).reshape(P, 2 * D),
        "scale16": over(f["L1_ffn_weight_scale"]),
        "mask8": np.ascontiguousarray(over(f["L1_ffn_weight_var_mask"].view(np.uint8))).view(np.int32),
        "biasF1": f["L1_ffn_bias"],
        "biasF3": f["L3_ffn_b_base"],
        "upF0": f["L0_ffn_lora_B"].transpose(0, 2, 1).reshape(2, 112, D).transpose(1, 0, 2),
        "upF2": f["L2_ffn_B"].transpose(0, 2, 1).reshape(64, 1, D),
        "upF3": f["L3_ffn_B_w"].T.reshape(16, 1, D),
        "cores": f["L3_ffn_cores"].reshape(128, 16),
    }
    arrays = {k: np.ascontiguousarray(v) for k, v in arrays.items()}
    nc = bacc.Bacc("TRN2", target_bir_lowering=False, num_devices=1)
    aps = {k: nc.dram_tensor(f"in_{k}", v.shape, mybir.dt.from_np(v.dtype), kind="ExternalInput").ap()
           for k, v in arrays.items()}
    aps["f1_store"] = nc.dram_tensor("f1_store", (P, KC * D), F32).ap()
    out = nc.dram_tensor("out_x", (TILES, P, D), F32, kind="ExternalOutput").ap()
    build(nc, aps, out)
    r = run_bass_kernel_spmd(nc, [{f"in_{k}": v for k, v in arrays.items()}], core_ids=[0])
    return r.results[0]["out_x"].reshape(B, S, D)
```

```python
from contextlib import ExitStack

import concourse.bass as bass
import numpy as np
from concourse import mybir

F32 = mybir.dt.float32
F32R = mybir.dt.float32r
F16 = mybir.dt.float16
I32 = mybir.dt.int32
U32 = mybir.dt.uint32
U8 = mybir.dt.uint8
ALU = mybir.AluOpType
ACT = mybir.ActivationFunctionType
AX_X = mybir.AxisListType.X

P = 128
B, S, D = 16, 64, 512
ROWS = B * S
TILES = ROWS // P
KC = D // P
HALVES = 2
HALF = ROWS // HALVES
HD = 128
HEADS = 32
GH = 4
UPW = 256
NEG = -1.0e30

C_ID, C_ONE, C_BLK, C_COS, C_SIN, C_IOTA, C_END = 0, 128, 256, 384, 448, 512, 544

GROUPS = HEADS // GH
W_L0Q, W_AG0, W_BASE0, W_L1Q = 0, 1, 2, 3
W_L1O = W_L1Q + 1
W_F1 = W_L1O + 2 * GROUPS - 1
W_L2Q = W_F1 + 1
W_L2O = W_L2Q + 1
W_AG2 = W_L2O + 2 * GROUPS - 1
W_L3Q = W_AG2 + 1
W_L3O = W_L3Q + 1
W_AG3 = W_L3O + 2 * GROUPS - 1
W_BASE3 = W_AG3 + 1
W_BLOCKS = W_BASE3 + 1
KV_BLOCKS = 8 + 8 + 4 + 1


class Layer:

    def __init__(self, name, subs, turns, w_o, kv):
        self.name, self.subs, self.turns = name, subs, turns
        self.w_o, self.kv = w_o, kv
        self.rope, self.norm, self.wide = name == "L1", name == "L2", name == "L3"
        self.keys = 2 * S if self.wide else S
        self.uses, self.pre, self.fill = [], [], []
        for sub in range(subs):
            q = [("q", sub, half, h) for half in range(HALVES) for h in range(GH)]
            wo = [("wo", sub, t) for t in range(TILES)]
            sq = lambda u: [("ss",) + u] if self.norm else []
            pre = []
            if sub == 0 and self.wide:
                pre = [("k", src, half) for src in range(2) for half in range(HALVES)]
                pre += [("v", 0, 0), ("v", 1, 0), q[0], ("vt", 0, 0), ("vt", 0, 1)]
                pre += [("v", 0, 1), ("v", 1, 1), q[1], ("vt", 1, 0), ("vt", 1, 1)]
                pre += [q[2], q[3], q[4]]
            elif sub == 0:
                pre = [("k", 0, 0), ("v", 0, 0), q[0]] + sq(("k", 0, 0)) + [("vt", 0, 0), q[1]] + sq(q[0])
                pre += [q[2]] + sq(q[1]) + [q[3]] + sq(q[2]) + [("k", 0, 1)] + sq(q[3]) + [q[4]] + sq(("k", 0, 1))
            else:
                pre = q[0:5]
            fill = [[q[5]] + sq(q[4]), [q[6]] + sq(q[5]), [q[7]] + sq(q[6]), sq(q[7]) + [wo[0]]]
            fill += [[w] for w in wo[1:]]
            if not self.wide:
                fill[0] = fill[0] + [("v", 0, 1)]
                fill[1] = fill[1][:1] + [("vt", 1, 0)] + fill[1][1:]
            self.pre.append(pre)
            self.fill.append(fill)
            for u in pre + [x for f in fill for x in f]:
                self.uses.append(u)
        n = len(self.uses)
        self.bank_of = [(i + 2) % 3 for i in range(n)]
        if self.bank_of[-1] == self.bank_of[0]:
            self.bank_of[-1] = self.bank_of[-3]
        self.n = n
        self.by_act = [u for u in self.uses if self.emptier(u) == "act"]
        self.by_dve = [u for u in self.uses if self.emptier(u) == "dve"]
        self.normed = [u for u in self.uses if u[0] == "ss"]
        self.roped = [u for u in self.uses if u[0] in "kq"]
        self.tiles = subs * TILES

    def emptier(self, use):
        if use[0] == "wo" or (self.rope and use[0] in "kq"):
            return "dve"
        return "act"

    def before(self, use):
        i = self.uses.index(use)
        for back in range(1, self.n + 1):
            if self.bank_of[(i - back) % self.n] == self.bank_of[i]:
                return self.uses[(i - back) % self.n], i - back < 0


L1 = Layer("L1", 1, 8, W_L1O, 0)
L2 = Layer("L2", 1, 8, W_L2O, 8)
L3 = Layer("L3", 2, 4, W_L3O, 16)


class Ffn:
    def __init__(self, name, base, bias, experts, rank, mix, scale):
        self.name, self.base, self.bias, self.experts, self.rank = name, base, bias, experts, rank
        self.mix, self.scale = mix, scale
        self.wide = experts * rank
        self.chunks = 2 if self.wide > P else 1
        self.chunk = self.wide // self.chunks if experts else 0
        self.out_lag = 4 if experts else 1
        self.add_lag = self.out_lag + 1
        self.next_lag = self.out_lag + 2
        self.out_banks = (4, 5) if experts else (4, 5, 6, 7)


F0 = Ffn("F0", True, False, 28, 8, False, 2.0)
F1 = Ffn("F1", True, True, 0, 0, False, 1.0)
F2 = Ffn("F2", False, False, 4, 16, False, 4.0)
F3 = Ffn("F3", True, True, 8, 16, True, 2.0)

JOBS = [(what, t) for t in range(TILES) for what in ("ctx", 0, "feat")]
for phase_, f_ in ((1, F0), (3, F1), (5, F2), (7, F3)):
    for i_ in range(TILES + f_.next_lag):
        if i_ < TILES:
            JOBS.append((phase_, i_))
        if phase_ < 7 and 0 <= i_ - f_.next_lag:
            JOBS.append((phase_ + 1, i_ - f_.next_lag))
JOB_BANK = [3 + t % 2 if what in (2, 4, 6) and t >= TILES - 2 else n % 2 for n, (what, t) in enumerate(JOBS)]
XN_ORDER = [job for job in JOBS if job[0] not in ("ctx", "feat")]
LN_ORDER = [(0, 0), (0, 1)]
for i_ in range(TILES + 4):
    LN_ORDER += [(1, i_ - 4)] if i_ >= 4 else []
    LN_ORDER += [(0, i_ + 2)] if i_ + 2 < TILES else []
LN_ORDER += [(phase_, t) for phase_ in range(2, 8) for t in range(TILES)]


def build(nc, a, out):
    with ExitStack() as ctx:
        def sb(name, cols, dt=F32):
            return ctx.enter_context(nc.sbuf_tensor(name, [P, cols], dt))

        def sem(name):
            return ctx.enter_context(nc.semaphore(name))

        ps = [ctx.enter_context(nc.psum_tensor(f"bank{i}", [P, 512], F32)) for i in range(8)]

        x_sb = sb("x_sb", TILES * D)
        x = x_sb[:, :].rearrange("p (t d) -> p t d", t=TILES)
        parts = {}
        for name in ("xT", "cT"):
            for part in ("hi", "lo"):
                parts[name, part] = sb(f"{name}_{part}", KC * ROWS, F32R)[:, :].rearrange("p (c r) -> p c r", c=KC)
        xT, cT = [[parts[n, p] for p in ("hi", "lo")] for n in ("xT", "cT")]
        w_raw = sb("w_raw", KC * D)
        wq_t = [sb(f"wq_{p}", KC * D, F32R) for p in ("hi", "lo")]
        wo_t = [sb(f"wo_{p}", KC * D, F32R) for p in ("hi", "lo")]
        wq = [w[:, :].rearrange("p (c n) -> p c n", c=KC) for w in wq_t]
        wo = [w[:, :].rearrange("p (c n) -> p c n", c=KC) for w in wo_t]
        kv_raw = sb("kv_raw", 2 * KC * HD)
        kv_t = [sb(f"kv_{p}", 2 * KC * HD, F32R) for p in ("hi", "lo")]
        wkv = [w[:, :].rearrange("p (s c n) -> p s c n", s=2, c=KC) for w in kv_t]
        q_sb = sb("q_sb", GH * ROWS)
        oT_t = [sb(f"oT_{p}", 4 * GH * P, F32R) for p in ("hi", "lo")]
        oT = [o[:, :].rearrange("p (s h r) -> p s h r", s=4, h=GH) for o in oT_t]
        k_sb = sb("k_sb", 2 * ROWS)
        vT_sb = sb("vT_sb", ROWS)
        v_sb = sb("v_sb", 2 * ROWS)
        s_sb = sb("s_sb", 2 * 512)
        pt_sb = sb("pt_sb", 2 * 512)
        m1_sb = sb("m1_sb", B * S)
        m2_sb = sb("m2_sb", S)
        squares = [sb(f"squares_{p}", 512, F32R)[:, :] for p in ("hi", "lo")]
        ones_r = sb("ones_r", P, F32R)[:, :]
        cst = sb("cst", C_END)
        small = sb("small", 192)
        stats = sb("stats", TILES * 6)
        idx8 = sb("idx8", 8, U32)

        ident = cst[:, C_ID:C_ID + P]
        ones = cst[:, C_ONE:C_ONE + P]
        blk = cst[:, C_BLK:C_BLK + P]
        iota = cst[:, C_IOTA:C_IOTA + 32]
        qT = q_sb[:, :].rearrange("p (b h r) -> p b h r", b=B, h=GH)
        mv = small[:, 0:16].rearrange("p (t s) -> p t s", s=2)
        rstd = small[:, 16:24]
        feat_ss = small[:, 24:32]
        feat_r = small[:, 32:40]
        mx = small[:, 40:48].rearrange("p (b j) -> p b j", b=2)
        sm = small[:, 48:56].rearrange("p (b j) -> p b j", b=2)
        rc = small[:, 56:64].rearrange("p (b j) -> p b j", b=2)
        eps5, eps6 = small[:, 64:65], small[:, 65:66]
        qk_w = small[:, 66:74]
        qk_raw = small[:, 74:84]
        ss0 = small[:, 84:88].rearrange("p (b j) -> p b j", b=2)
        r0 = small[:, 88:92].rearrange("p (b j) -> p b j", b=2)
        lg = small[:, 92:124]
        top8 = small[:, 124:132]
        idxf = small[:, 132:134]
        gate_d, gate_e, gate_a, gate_r = [small[:, 134 + i:135 + i] for i in range(4)]
        gate_p2 = small[:, 139:140]
        g1 = small[:, 140:168]
        c_nat = q_sb[:, :].rearrange("p (t d) -> p t d", t=TILES)
        qk_rows = k_sb[:, :].rearrange("p (b s d) -> p b s d", b=2, s=2)
        bq_row, bk_row, fn_row, ctx_squares = [v_sb[:, i * D:(i + 1) * D] for i in range(4)]
        qk_squares = m1_sb[:, :].rearrange("p (s d) -> p s d", s=2)
        wk_raw = k_sb[:, :]
        QT0, KT0 = [vT_sb[:, i * D:(i + 1) * D].rearrange("p (c r) -> p c r", c=KC) for i in range(2)]
        up_w = k_sb[:, 0:2 * D].rearrange("p (c d) -> p c d", c=2)
        cores = k_sb[:, 2 * D:2 * D + 16]
        bias_row = v_sb[:, 0:D]
        hm = q_sb[:, 0:512].rearrange("p (b n) -> p b n", b=2)
        hT = q_sb[:, 512:1536].rearrange("p (b c r) -> p b c r", b=4, c=2)
        mT = q_sb[:, 1536:1792].rearrange("p (b r) -> p b r", b=2)
        xn = s_sb[:, :].rearrange("p (b d) -> p b d", b=2)
        raw_squares = [v_sb[:, ROWS + b * HALF:ROWS + (b + 1) * HALF] for b in range(2)]
        soft0 = [pt_sb[:, b * 512 + P:b * 512 + 2 * P] for b in range(2)]
        packed = q_sb[:, 1536:2560].bitcast(I32)
        nib = q_sb[:, 2560:3584].bitcast(I32)
        scale16 = q_sb[:, 3584:4096].bitcast(F16)
        mask_words = k_sb[:, 1040:1296].bitcast(I32)
        mask8 = mask_words.bitcast(U8)
        nibf = [v_sb[:, i * ROWS:(i + 1) * ROWS] for i in range(2)]
        sc_f = vT_sb[:, :]

        s_ident, s_fn, s_const, ones_ready = sem("tables_loaded"), sem("fn_loaded"), sem("consts_loaded"), sem("ones_ready")
        s_eps = sem("eps_written")
        s_x = [sem(f"x_loaded_{t}") for t in range(TILES)]
        s_ctx = [sem(f"ctx_loaded_{t}") for t in range(TILES)]
        wk_loaded, wk_hi = sem("wk_loaded"), sem("wk_hi")
        dve_split = sem("dve_split")

        s_mask = sem("masks_loaded")
        s_out = sem("out_stored")
        w_loaded, w_hi, w_split = sem("w_loaded"), sem("w_hi"), sem("w_split")
        kv_loaded, kv_hi, kv_split = sem("kv_loaded"), sem("kv_hi"), sem("kv_split")
        tr_full, tr_hi, tr_lo = sem("tr_full"), sem("tr_hi"), sem("tr_lo")
        ln_var, ln_tmp, ln_rstd, xn_ready = sem("ln_var"), sem("ln_tmp"), sem("ln_rstd"), sem("xn_ready")
        dve_step = sem("dve_step")
        act_step = sem("act_step")
        x_added = sem("x_added")
        extra_loaded = sem("extra_loaded")
        bias_added = sem("bias_added")
        f1_loaded, f1_ready, f1_stored = sem("f1_loaded"), sem("f1_ready"), sem("f1_stored")

        z = {k: sem(f"L0_{k}") for k in ("ss_c r_c feat qk_full qb ss qn qkt_full qkt_q qkt_k s_full s_read "
                                         "exp p_ready pt_full pt_ready av_full").split()}

        def layer_sems(lay):
            names = "full ev_act ev_dve s_full s_read s_max s_shift exp s_sum s_rec p_ready t_full pt_ready o_full o_hi o_lo"
            names += " roped" if lay.rope else ""
            names += " copied r_ready normed sq_raw sq_lo" if lay.norm else ""
            made = {k: sem(f"{lay.name}_{k}") for k in names.split()}
            per = {k: lay.tiles for k in made}
            per.update(full=lay.n, ev_act=len(lay.by_act), ev_dve=len(lay.by_dve))
            per.update(roped=len(lay.roped))
            per.update({k: len(lay.normed) for k in ("copied", "r_ready", "normed", "sq_raw", "sq_lo")})
            return made, per

        big = {lay.name: layer_sems(lay) for lay in (L1, L2, L3)}
        ffn = {}
        for f in (F0, F1, F2, F3):
            names = "b_full" + (" g_full d e hm_ready ht_full ht_ready" if f.experts else "") + (" mx_full mx_ready" if f.mix else "")
            ffn[f.name] = {k: sem(f"{f.name}_{k}") for k in names.split()}
        added_before = {"L0": 0, "F0": 8, "F1": 16, "F2": 24, "F3": 32}

        def done(lay, name, turn, k):
            per = big[lay.name][1][name]
            return turn * per + (per + k)

        def prime(eng, lay, names):
            for k in names.split():
                if k in big[lay.name][0]:
                    eng.sem_inc(big[lay.name][0][k], big[lay.name][1][k])

        def batches(ap):
            return ap.rearrange("p (b r) -> p b r", r=S)

        rope_terms = [[area[:, ROWS + i * HALF:ROWS + (i + 1) * HALF] for i in range(2)] for area in (k_sb, v_sb)]

        def place_of(use):
            if use[0] == "k":
                return batches(k_sb[:, use[2] * HALF:(use[2] + 1) * HALF])
            return qT[:, 8 * use[2]:8 * use[2] + 8, use[3], :]

        def job(what, t):
            return JOBS.index((what, t))

        def by_chunk(cols):
            return lambda w: w[:, :].rearrange("p (c n) -> p c n", c=KC)[:, :, cols]

        block = ctx.enter_context(nc.Block())

        @block.sync
        def _(sp):
            for t in range(TILES):
                sp.dma_start(c_nat[:, t, :], a["ctx"][:, t, :]).then_inc(s_ctx[t], 16)
                sp.dma_start(x[:, t, :], a["x"][:, t, :]).then_inc(s_x[t], 16)
                if t == 0:
                    sp.dma_start(w_raw[:, :], a["w"][W_L0Q]).then_inc(w_loaded, 16)
                if t == 1:
                    sp.dma_start(wk_raw, a["wk"]).then_inc(wk_loaded, 16)
            sp.dma_start(kv_raw[:, :], a["kv"][0]).then_inc(kv_loaded, 16)

            def load_w(n, block_):
                sp.wait_ge(w_split, n)
                sp.dma_start(w_raw[:, :], block_).then_inc(w_loaded, 16)

            sp.wait_ge(dve_split, 1)
            load_w(W_AG0, a["w"][W_AG0])
            load_w(W_BASE0, a["w"][W_BASE0])
            sp.wait_ge(x_added, TILES)
            sp.dma_start(up_w[0:112, :, :], a["upF0"]).then_inc(extra_loaded, 16)
            sp.dma_start(packed, a["packed"]).then_inc(f1_loaded, 16)
            sp.dma_start(scale16, a["scale16"]).then_inc(f1_loaded, 16)
            sp.dma_start(mask_words, a["mask8"]).then_inc(f1_loaded, 16)
            sp.dma_start(m1_sb[:, :], a["m1"]).then_inc(s_mask, 16)
            sp.dma_start(m2_sb[:, :], a["m2"]).then_inc(s_mask, 16)
            with sp.Fori(W_BASE0 + 1, W_F1) as n:
                load_w(n, a["w"][bass.ds(n, 1), :, :].rearrange("a p n -> (a p) n"))
            sp.wait_ge(f1_stored, 32)
            load_w(W_F1, a["f1_store"])
            with sp.Fori(W_F1 + 1, W_BLOCKS) as n:
                load_w(n, a["w"][bass.ds(n - 1, 1), :, :].rearrange("a p n -> (a p) n"))
            for t in range(TILES):
                sp.wait_ge(x_added, added_before["F3"] + t + 1)
                sp.dma_start(out[t], x[:, t, :]).then_inc(s_out, 16)
            sp.wait_ge(s_out, 16 * TILES)

        @block.gpsimd
        def _(pool):
            pool.memset(eps5, 1e-5)
            pool.memset(eps6, 1e-6).then_inc(s_eps, 1)

            def low_narrow(n, dst):
                pool.wait_ge(w_hi, n + 1)
                for c in range(0, KC, 2):
                    cols = lambda w: by_chunk(slice(0, UPW))(w)[:, c:c + 2, :]
                    last = nc.gpsimd.tensor_tensor(cols(dst[1]), cols(w_raw), cols(dst[0]).bitcast(F32), ALU.subtract)
                last.then_inc(w_split, 1)

            def low_w(n, dst, chunks=KC):
                pool.wait_ge(w_hi, n + 1)
                for c in range(chunks):
                    cols = slice(c * 512, (c + 1) * 512)
                    last = nc.gpsimd.tensor_tensor(dst[1][:, cols], w_raw[:, cols], dst[0][:, cols].bitcast(F32), ALU.subtract)
                last.then_inc(w_split, 1)

            def low_kv(n):
                pool.wait_ge(kv_hi, n + 1)
                for c in range(2):
                    cols = slice(c * 512, (c + 1) * 512)
                    last = nc.gpsimd.tensor_tensor(kv_t[1][:, cols], kv_raw[:, cols], kv_t[0][:, cols].bitcast(F32), ALU.subtract)
                last.then_inc(kv_split, 1)

            low_w(W_L0Q, wq_t, 2)
            low_kv(0)
            low_narrow(W_AG0, wq_t)
            low_w(W_BASE0, wo_t)
            low_w(W_L1Q, wq_t)

            def rope_sums(lay, g, uses):
                own = big[lay.name][0]
                for use in uses:
                    if use not in lay.roped:
                        continue
                    pool.wait_ge(own["ev_dve"], done(lay, "ev_dve", g, lay.by_dve.index(use) + 1))
                    ta, tb = rope_terms[lay.roped.index(use) % 2]
                    nc.gpsimd.tensor_tensor(place_of(use), batches(ta), batches(tb), ALU.add).then_inc(own["roped"], 1)

            def add_bias(phase, extra):
                for t in range(TILES):
                    pool.wait_ge(xn_ready, XN_ORDER.index((phase, t)) + 1)
                    pool.wait_ge(extra_loaded, extra)
                    nc.gpsimd.tensor_tensor(x[:, t, :], x[:, t, :], bias_row, ALU.add).then_inc(bias_added, 1)

            for lay in (L1, L2, L3):
                prime(pool, lay, "roped")
                with pool.Fori(0, lay.turns) as g:
                    for sub in range(lay.subs):
                        n = g * (2 * lay.subs) + 2 * sub
                        if lay.rope:
                            rope_sums(lay, g, lay.pre[sub][:5])
                            low_w(n + lay.w_o, wo_t)
                            rope_sums(lay, g, lay.pre[sub][5:] + [u for fill in lay.fill[sub] for u in fill])
                            low_w(n + (lay.w_o + 1), wq_t)
                            low_kv(g + (lay.kv + 1))
                            continue
                        low_w(n + lay.w_o, wo_t)
                        low_w(n + (lay.w_o + 1), wq_t)
                        if sub == lay.subs - 1:
                            low_kv(g + (lay.kv + 1))
                if lay is L1:
                    add_bias(3, 16 * (1 + 1))
                if lay is not L3:
                    low_w(W_L2Q if lay is L1 else W_L3Q, wq_t)
            low_w(W_BASE3, wo_t)
            add_bias(7, 16 * (1 + 1 + 1 + 3))

        @block.scalar
        def _(act):
            steps = [0]

            def step(ins):
                steps[0] += 1
                ins.then_inc(act_step, 1)
                act.wait_ge(act_step, steps[0])

            def high_w(n, dst, width=D):
                act.wait_ge(w_loaded, n * 16 + 16)
                cols = by_chunk(slice(0, width))
                nc.scalar.activation(cols(dst[0]), cols(w_raw), ACT.Copy).then_inc(w_hi, 1)

            def high_w_piece(n, dst, piece):
                if piece == 0:
                    act.wait_ge(w_loaded, n * 16 + 16)
                cols = slice(piece * D, (piece + 1) * D)
                ins = nc.scalar.activation(dst[0][:, cols], w_raw[:, cols], ACT.Copy)
                if piece == KC - 1:
                    ins.then_inc(w_hi, 1)

            def high_kv(n):
                act.wait_ge(kv_loaded, n * 16 + 16)
                nc.scalar.activation(kv_t[0][:, :], kv_raw[:, :], ACT.Copy).then_inc(kv_hi, 1)

            def high_turned(what, t, dst):
                n = job(what, t)
                act.wait_ge(tr_full, n + 1)
                nc.scalar.activation(dst, ps[JOB_BANK[n]][:, :].rearrange("p (c r) -> p c r", c=KC), ACT.Copy).then_inc(tr_hi, 1)

            def rows_of(parts_, t):
                return parts_[0][:, :, t * P:(t + 1) * P]

            def norm_x(phase, t):
                n = LN_ORDER.index((phase, t)) + 1
                act.wait_ge(ln_var, n)
                nc.scalar.activation(rstd[:, t:t + 1], mv[:, t, 1:2], ACT.Ln, bias=eps5).then_inc(ln_tmp, 1)
                act.wait_ge(ln_tmp, n)
                nc.scalar.activation(rstd[:, t:t + 1], rstd[:, t:t + 1], ACT.Exp, scale=-0.5).then_inc(ln_rstd, 1)

            nc.scalar.preload_act_table_set("natural_log_exp_and_others")
            act.dma_start(cst[:, :], a["cst"]).then_inc(s_ident, 16)
            act.dma_start(fn_row, a["fn"].partition_broadcast(P)).then_inc(s_fn, 16)
            act.dma_start(qk_raw, a["qkw"]).then_inc(s_const, 16)
            for row, name in ((bq_row, "bq"), (bk_row, "bk")):
                act.dma_start(row, a[name].partition_broadcast(P)).then_inc(s_const, 16)

            def gate_exp(f, count):
                fs = ffn[f.name]
                act.wait_ge(fs["d"], count)
                if f.mix:
                    nc.scalar.activation(g1[:, 0:f.experts], g1[:, 0:f.experts], ACT.Exp, accum_out=gate_a).then_inc(fs["e"], 1)
                else:
                    nc.scalar.activation(gate_e, gate_d, ACT.Exp).then_inc(fs["e"], 1)

            def l0_feature_norm(t):
                act.wait_ge(s_ctx[t], 16)
                nc.scalar.activation(ctx_squares, c_nat[:, t, :], ACT.Square, accum_out=feat_ss[:, t:t + 1]).then_inc(z["ss_c"], 1)
                act.wait_ge(z["ss_c"], t + 1)
                step(nc.scalar.activation(feat_r[:, t:t + 1], feat_ss[:, t:t + 1], ACT.Ln, scale=1.0 / D, bias=eps6))
                nc.scalar.activation(feat_r[:, t:t + 1], feat_r[:, t:t + 1], ACT.Exp, scale=-0.5).then_inc(z["r_c"], 1)

            act.wait_ge(s_eps, 1)
            l0_feature_norm(0)
            act.wait_ge(s_ident, 16)
            nc.scalar.activation(ones_r, ones, ACT.Copy).then_inc(ones_ready, 1)
            high_turned("ctx", 0, rows_of(cT, 0))
            norm_x(0, 0)
            high_turned(0, 0, rows_of(xT, 0))
            high_turned("feat", 0, oT[0][:, 0, :, :])
            l0_feature_norm(1)
            norm_x(0, 1)
            high_w(W_L0Q, wq_t)
            act.wait_ge(wk_loaded, 16)
            nc.scalar.activation(wo_t[0][:, :], wk_raw, ACT.Copy).then_inc(wk_hi, 1)

            for i in range(TILES + 4):
                if i + 1 < TILES:
                    high_turned("ctx", i + 1, rows_of(cT, i + 1))
                    high_turned(0, i + 1, rows_of(xT, i + 1))
                if i in (TILES, TILES + 1):
                    high_turned(1, i - TILES, rows_of(xT, i - TILES))
                if i == TILES:
                    act.wait_ge(z["qk_full"], 2 * TILES)
                    high_w(W_AG0, wq_t, UPW)
                if i == TILES + 3:
                    gate_exp(F0, 1)
                if 0 <= i - 4 < TILES:
                    norm_x(1, i - 4)
                if i + 2 < TILES:
                    l0_feature_norm(i + 2)
                    norm_x(0, i + 2)
                if 0 <= i - 3 < TILES:
                    t = i - 3
                    act.wait_ge(z["pt_full"], t + 1)
                    if t >= 2:
                        act.wait_ge(z["av_full"], t - 1)
                    nc.scalar.activation(pt_sb[:, (t % 2) * 512:(t % 2) * 512 + P], ps[6][:, P:2 * P], ACT.Copy).then_inc(z["pt_ready"], 1)
                if i < TILES:
                    for j in range(2):
                        act.wait_ge(z["qb"], 2 * i + j + 1)
                        nc.scalar.activation(qk_squares[:, j, :], qk_rows[:, i % 2, j, :], ACT.Square,
                                             accum_out=ss0[:, i % 2, j:j + 1]).then_inc(z["ss"], 1)
                    if i + 1 < TILES:
                        high_turned("feat", i + 1, oT[0][:, (i + 1) % 4, :, :])
                    act.wait_ge(z["ss"], 2 * i + 2)
                    step(nc.scalar.activation(r0[:, i % 2, :], ss0[:, i % 2, :], ACT.Ln, scale=1.0 / D, bias=eps6))
                    step(nc.scalar.activation(r0[:, i % 2, :], r0[:, i % 2, :], ACT.Exp, scale=-0.5))
                if 0 <= i - 2 < TILES:
                    t = i - 2
                    act.wait_ge(z["s_read"], 3 * (t + 1))
                    nc.scalar.activation(soft0[t % 2], soft0[t % 2], ACT.Exp, accum_out=sm[:, t % 2, 0:1]).then_inc(z["exp"], 1)
                if i < TILES:
                    for j in range(2):
                        nc.scalar.activation(qk_rows[:, i % 2, j, :], qk_rows[:, i % 2, j, :], ACT.Copy,
                                             scale=r0[:, i % 2, j:j + 1]).then_inc(z["qn"], 1)
                if 0 <= i - 1 < TILES:
                    t = i - 1
                    act.wait_ge(z["qkt_full"], t + 1)
                    if t >= 1:
                        act.wait_ge(z["s_full"], t)
                    nc.scalar.activation(QT0, ps[4][:, :].rearrange("p (c r) -> p c r", c=KC), ACT.Copy).then_inc(z["qkt_q"], 1)
                if i == 2:
                    high_kv(0)

            def ffn_act(f, phase):
                fs = ffn[f.name]
                for i in range(TILES + f.next_lag + 1):
                    if i == TILES + 1 and f is F1:
                        act.wait_ge(fs["b_full"], TILES)
                        high_w(W_L2Q, wq_t)
                    if 0 <= i - f.next_lag - 1 < TILES and f is not F3:
                        high_turned(phase + 1, i - f.next_lag - 1, rows_of(xT, i - f.next_lag - 1))
                    if i < TILES and (i >= 2 or f is not F0):
                        high_turned(phase, i, rows_of(xT, i))
                    if i < 2 and f is not F0:
                        norm_x(phase, TILES - 2 + i)
                    if (1 if f is F0 else 0) <= i - 1 < TILES and f.experts:
                        gate_exp(f, i)
                    if 0 <= i - f.add_lag < TILES and f is not F3:
                        norm_x(phase + 1, i - f.add_lag)
                    if 0 <= i - 2 < TILES and f.experts:
                        t = i - 2
                        act.wait_ge(fs["ht_full"], t + 1)
                        if t >= 4:
                            act.wait_ge(fs["b_full"], t - 3)
                        src = ps[6][0:f.chunk, 0:f.chunks * P].rearrange("p (c r) -> p c r", c=f.chunks)
                        nc.scalar.activation(hT[0:f.chunk, t % 4, 0:f.chunks, :], src, ACT.Copy,
                                             scale=1.0 if f.mix else f.scale).then_inc(fs["ht_ready"], 1)
                    if 0 <= i - 3 < TILES and f.mix:
                        t = i - 3
                        act.wait_ge(fs["mx_full"], t + 1)
                        if t >= 2:
                            act.wait_ge(fs["b_full"], t - 1)
                        nc.scalar.activation(mT[0:16, t % 2, :], ps[7][0:16, 0:P], ACT.Copy, scale=f.scale).then_inc(fs["mx_ready"], 1)
                    if i == (2 if f is F0 else 1) and f in (F0, F3):
                        high_w(W_BASE0 if f is F0 else W_BASE3, wo_t)
                    if f is F0 and i in (8, 11):
                        part = (i - 8) // 3
                        act.wait_ge(f1_ready, part + 1)
                        store = a["f1_store"].rearrange("p (c s n) -> p c s n", c=2, s=2)[:, :, part, :]
                        act.dma_start(store, nibf[part].rearrange("p (c n) -> p c n", c=2)).then_inc(f1_stored, 16)
                    if i == TILES and f in (F0, F2):
                        act.wait_ge(fs["g_full"], TILES)
                        high_w(W_L1Q if f is F0 else W_L3Q, wq_t)

            def load_extra(f):
                if f.experts:
                    src = a[f"up{f.name}"]
                    act.dma_start(up_w[0:src.shape[0], 0:src.shape[1], :], src).then_inc(extra_loaded, 16)
                if f.mix:
                    act.dma_start(cores, a["cores"]).then_inc(extra_loaded, 16)
                if f.bias:
                    act.dma_start(bias_row, a[f"bias{f.name}"].partition_broadcast(P)).then_inc(extra_loaded, 16)

            act.wait_ge(x_added, TILES)
            ffn_act(F0, 1)
            act.wait_ge(x_added, 2 * TILES)
            act.wait_ge(f1_stored, 32)

            def attend(lay, phase):
                own, per = big[lay.name]
                prime(act, lay, "ev_act exp pt_ready o_hi r_ready copied")
                scale = 1.0 if not lay.wide else float(HD) ** -0.5

                def turn(g, last):
                    def wait(name, k):
                        act.wait_ge(own[name], done(lay, name, g, k))

                    def full(use):
                        wait("full", lay.uses.index(use) + 1)

                    def empty(use):
                        if lay.emptier(use) != "act":
                            return
                        full(use)
                        bank = ps[lay.bank_of[lay.uses.index(use)]]
                        kind = use[0]
                        if kind in "kv":
                            src, half = (use[1], use[2]) if lay.wide else (0, use[2])
                            if lay.wide:
                                inp = bank[:, :].rearrange("p (b r) -> p b r", r=S)
                                area = (k_sb if kind == "k" else vT_sb)[:, :].rearrange("p (b r) -> p b r", r=2 * S)
                                first = 8 * half if kind == "k" else 0
                                dst = area[:, first:first + 8, src * S:(src + 1) * S]
                                if kind == "v" and half == 1:
                                    full(("vt", 0, 1))
                            else:
                                inp, dst = bank[:, :], (k_sb if kind == "k" else vT_sb)[:, half * HALF:(half + 1) * HALF]
                        elif kind == "vt":
                            at = (2 * use[1] + use[2]) if lay.wide else use[1]
                            inp, dst = bank[:, :], v_sb[:, at * 512:(at + 1) * 512]
                        elif kind == "q":
                            inp, dst = bank[:, :].rearrange("p (b r) -> p b r", r=S), qT[:, 8 * use[2]:8 * use[2] + 8, use[3], :]
                        else:
                            m = lay.normed.index(use)
                            r = m1_sb[:, (m % 2) * 512:(m % 2) * 512 + 512]
                            wait("normed", m - 1)
                            nc.scalar.activation(r, bank[:, :], ACT.Ln, scale=1.0 / HD, bias=eps5).then_inc(own["ev_act"], 1)
                            wait("ev_act", lay.by_act.index(use) + 1)
                            nc.scalar.activation(r, r, ACT.Exp, scale=-0.5).then_inc(own["r_ready"], 1)
                            return
                        ins = nc.scalar.activation(dst, inp, ACT.Copy)
                        if lay.norm and kind in "kq":
                            m = lay.normed.index(("ss",) + use)
                            ins.then_inc(own["copied"], 1)
                            before = lay.normed[m - 1]
                            wait("full", lay.uses.index(before) + 1 - (lay.n if m < 1 else 0))
                            nc.scalar.activation(squares[0], bank[:, :], ACT.Square).then_inc(own["ev_act"], 1)
                            return
                        ins.then_inc(own["ev_act"], 1)

                    for sub in range(lay.subs):
                        n = g * (2 * lay.subs) + 2 * sub
                        first = 0 if sub else lay.pre[0].index(("vt", 0, 0))
                        for at, use in enumerate(lay.pre[sub]):
                            if at == first:
                                if sub:
                                    full(("wo", sub - 1, TILES - 1))
                                else:
                                    wait("full", 0)
                            empty(use)
                            if 0 <= at - first < KC:
                                high_w_piece(n + lay.w_o, wo_t, at - first)
                        for i in range(len(lay.fill[sub])):
                            if 1 <= i:
                                for use in lay.fill[sub][i - 1]:
                                    empty(use)
                            if 0 <= i - 1 < TILES:
                                t = sub * TILES + i - 1
                                wait("t_full", t + 1)
                                wait("o_full", t - 1)
                                w = 4 * lay.keys
                                nc.scalar.activation(pt_sb[:, (t % 2) * 512:(t % 2) * 512 + w], ps[5][:, 0:w], ACT.Copy)\
                                    .then_inc(own["pt_ready"], 1)
                            if i < TILES:
                                t = sub * TILES + i
                                wait("s_shift", t + 1)
                                w = 4 * lay.keys
                                sv = s_sb[:, (t % 2) * 512:(t % 2) * 512 + w]
                                nc.scalar.activation(sv, sv, ACT.Exp, scale=scale).then_inc(own["exp"], 1)
                            if 0 <= i - 2 < TILES:
                                t = sub * TILES + i - 2
                                wait("o_full", t + 1)
                                if i - 2 >= 4:
                                    full(("wo", sub, i - 6))
                                elif sub:
                                    full(("wo", sub - 1, i + 2))
                                else:
                                    wait("full", lay.uses.index(("wo", lay.subs - 1, i + 2)) + 1 - lay.n)
                                for b in range(2):
                                    ins = nc.scalar.activation(oT[0][:, t % 4, :, b * S:(b + 1) * S],
                                                               ps[6 + b][:, 0:GH * S].rearrange("p (h r) -> p h r", h=GH), ACT.Copy)
                                ins.then_inc(own["o_hi"], 1)
                            if i == 0 and sub == 0:
                                kv_next(g + (lay.kv + 1))
                            if i == 6 and sub == lay.subs - 1:
                                high_kv(g + (lay.kv + 1))
                            if i == 4:
                                full(("q", sub, 1, GH - 1))
                            if 0 <= i - 4 < KC:
                                high_w_piece(n + (lay.w_o + 1), wq_t, i - 4)
                            if last and sub == lay.subs - 1 and 0 <= i - 5:
                                norm_x(phase + 1, i - 5)

                with act.Fori(0, lay.turns - 1) as g:
                    turn(g, False)
                turn(lay.turns - 1, True)

            def kv_next(n):
                act.wait_ge(kv_split, n)
                act.dma_start(kv_raw[:, :], a["kv"][bass.ds(n, 1), :, :].rearrange("a p n -> (a p) n")).then_inc(kv_loaded, 16)

            attend(L1, 2)

            act.wait_ge(big["L1"][0]["ev_dve"], done(L1, "ev_dve", L1.turns - 1, len(L1.by_dve)))
            load_extra(F1)
            ffn_act(F1, 3)
            act.wait_ge(x_added, 3 * TILES)
            attend(L2, 4)
            act.wait_ge(big["L2"][0]["ev_dve"], done(L2, "ev_dve", L2.turns - 1, len(L2.by_dve)))
            load_extra(F2)
            ffn_act(F2, 5)
            act.wait_ge(x_added, 4 * TILES)
            attend(L3, 6)
            act.wait_ge(big["L3"][0]["ev_dve"], done(L3, "ev_dve", L3.turns - 1, len(L3.by_dve)))
            load_extra(F3)
            ffn_act(F3, 7)

        @block.vector
        def _(dve):
            steps = [0]

            def step(ins):
                steps[0] += 1
                ins.then_inc(dve_step, 1)
                return ins

            def settle():
                dve.wait_ge(dve_step, steps[0])

            def low_turned(what, t, dst):
                n = job(what, t)
                dve.wait_ge(tr_hi, n + 1)
                nc.vector.tensor_tensor(dst[1], ps[JOB_BANK[n]][:, :].rearrange("p (c r) -> p c r", c=KC), dst[0].bitcast(F32),
                                        ALU.subtract).then_inc(tr_lo, 1)

            def rows_of(parts_, t):
                return [p[:, :, t * P:(t + 1) * P] for p in parts_]

            def mean_var(t):
                step(nc.vector.bn_stats(stats[:, 6 * t:6 * t + 6], x[:, t, :]))
                settle()
                nc.vector.bn_aggr(mv[:, t, :], stats[:, 6 * t:6 * t + 6]).then_inc(ln_var, 1)

            def norm_x(phase, t):
                n = XN_ORDER.index((phase, t))
                dve.wait_ge(ln_rstd, LN_ORDER.index((phase, t)) + 1)
                if n >= 2:
                    dve.wait_ge(tr_full, job(*XN_ORDER[n - 2]) + 1)
                nc.vector.tensor_scalar(xn[:, n % 2, :], x[:, t, :], mv[:, t, 0:1], rstd[:, t:t + 1],
                                        ALU.subtract, ALU.mult).then_inc(xn_ready, 1)

            def gates_top2(f, t, fs, bank):
                e, w = f.experts, f.wide
                if e < 8:
                    step(nc.vector.tensor_copy(lg[:, 0:e], bank[:, w:w + e]))
                    settle()
                    logits = lg[:, 0:8]
                else:
                    logits = bank[:, w:w + e]
                step(nc.vector.max(top8, logits))
                settle()
                step(nc.vector.max_index(idx8[:, :], top8, logits))
                nc.vector.tensor_tensor(gate_d, top8[:, 1:2], top8[:, 0:1], ALU.subtract).then_inc(fs["d"], 1)
                settle()
                step(nc.vector.tensor_copy(idxf, idx8[:, 0:2]))

            def weights_top2(f, t, fs, bank):
                e, w = f.experts, f.wide
                dve.wait_ge(fs["e"], t + 1)
                step(nc.vector.tensor_scalar(gate_a, gate_e, 1.0, None, ALU.add))
                settle()
                step(nc.vector.reciprocal(gate_r, gate_a))
                settle()
                step(nc.vector.tensor_tensor(gate_p2, gate_r, gate_e, ALU.mult))
                step(nc.vector.tensor_scalar(g1[:, 0:e], iota[:, 0:e], idxf[:, 0:1], gate_r, ALU.is_equal, ALU.mult))
                settle()
                step(nc.vector.tensor_scalar(lg[:, 0:e], iota[:, 0:e], idxf[:, 1:2], gate_p2, ALU.is_equal, ALU.mult))
                settle()
                step(nc.vector.tensor_tensor(g1[:, 0:e], g1[:, 0:e], lg[:, 0:e], ALU.add))
                settle()
                nc.vector.tensor_tensor(hm[:, t % 2, 0:w].rearrange("p (e r) -> p e r", e=e),
                                        bank[:, 0:w].rearrange("p (e r) -> p e r", e=e),
                                        g1[:, 0:e].unsqueeze(2).to_broadcast([P, e, f.rank]), ALU.mult).then_inc(fs["hm_ready"], 1)

            def gates_all(f, t, fs, bank):
                e, r = f.experts, f.rank
                step(nc.vector.tensor_reduce(gate_d, bank[:, r:r + e], AX_X, ALU.max))
                settle()
                nc.vector.tensor_scalar(g1[:, 0:e], bank[:, r:r + e], gate_d, None, ALU.subtract).then_inc(fs["d"], 1)
                step(nc.vector.tensor_copy(lg[:, 0:r], bank[:, 0:r]))

            def weights_all(f, t, fs, bank):
                e, r = f.experts, f.rank
                dve.wait_ge(fs["e"], t + 1)
                step(nc.vector.reciprocal(gate_r, gate_a))
                settle()
                step(nc.vector.tensor_scalar(g1[:, 0:e], g1[:, 0:e], gate_r, None, ALU.mult))
                settle()
                nc.vector.tensor_tensor(hm[:, t % 2, 0:e * r].rearrange("p (e r) -> p e r", e=e),
                                        lg[:, 0:r].unsqueeze(1).to_broadcast([P, e, r]),
                                        g1[:, 0:e].unsqueeze(2).to_broadcast([P, e, r]), ALU.mult).then_inc(fs["hm_ready"], 1)

            def l0_feature(t):
                dve.wait_ge(z["r_c"], t + 1)
                dve.wait_ge(tr_full, job("ctx", t) + 1)
                nc.vector.scalar_tensor_tensor(out=c_nat[:, t, :], in0=c_nat[:, t, :], scalar=feat_r[:, t:t + 1], in1=fn_row,
                                               op0=ALU.mult, op1=ALU.mult).then_inc(z["feat"], 1)

            def l0_mean_var(t):
                dve.wait_ge(s_x[t], 16)
                mean_var(t)

            l0_mean_var(0)
            norm_x(0, 0)
            low_turned("ctx", 0, rows_of(cT, 0))
            dve.wait_ge(s_ident, 16)
            dve.wait_ge(s_fn, 16)
            l0_feature(0)
            low_turned(0, 0, rows_of(xT, 0))
            low_turned("feat", 0, [o[:, 0, :, :] for o in oT])
            l0_mean_var(1)
            norm_x(0, 1)
            dve.wait_ge(s_const, 3 * 16)
            step(nc.vector.tensor_tensor(qk_w[:, 0:4], qk_raw[:, 0:4], qk_raw[:, 4:8], ALU.mult))
            step(nc.vector.tensor_tensor(qk_w[:, 4:5], qk_raw[:, 8:9], qk_raw[:, 9:10], ALU.mult))
            dve.wait_ge(w_hi, 1)
            half = slice(2 * D, 4 * D)
            nc.vector.tensor_tensor(wq_t[1][:, half], w_raw[:, half], wq_t[0][:, half].bitcast(F32), ALU.subtract).then_inc(dve_split, 1)
            dve.wait_ge(wk_hi, 1)
            nc.vector.tensor_tensor(wo_t[1][:, :], wk_raw, wo_t[0][:, :].bitcast(F32), ALU.subtract).then_inc(dve_split, 1)
            dve.wait_ge(dve_split, 2)
            for i in range(TILES + 4):
                if i == TILES + 3:
                    dve.wait_ge(ffn["F0"]["g_full"], 1)
                    gates_top2(F0, 0, ffn["F0"], ps[2])
                    weights_top2(F0, 0, ffn["F0"], ps[2])
                if 0 <= i - 4 < TILES:
                    t = i - 4
                    dve.wait_ge(z["av_full"], t + 1)
                    nc.vector.tensor_tensor(x[:, t, :], ps[7][:, :], x[:, t, :], ALU.add).then_inc(x_added, 1)
                    dve.wait_ge(x_added, t + 1)
                    mean_var(t)
                if i + 2 < TILES:
                    l0_mean_var(i + 2)
                if i + 1 < TILES:
                    low_turned("ctx", i + 1, rows_of(cT, i + 1))
                    l0_feature(i + 1)
                    low_turned(0, i + 1, rows_of(xT, i + 1))
                if TILES <= i < TILES + 2:
                    low_turned(1, i - TILES, rows_of(xT, i - TILES))
                if i < TILES:
                    for j in range(2):
                        dve.wait_ge(z["qk_full"], 2 * i + j + 1)
                        if i >= 2:
                            dve.wait_ge(z["qkt_full"], i - 1)
                        nc.vector.tensor_tensor(qk_rows[:, i % 2, j, :], ps[2 + j][:, :], (bq_row, bk_row)[j], ALU.add)\
                            .then_inc(z["qb"], 1)
                if i + 1 < TILES:
                    low_turned("feat", i + 1, [o[:, (i + 1) % 4, :, :] for o in oT])
                if i + 2 < TILES:
                    norm_x(0, i + 2)
                if 0 <= i - 2 < TILES:
                    t = i - 2
                    sv = soft0[t % 2]
                    dve.wait_ge(z["s_full"], t + 1)
                    if t >= 2:
                        dve.wait_ge(z["pt_full"], t - 1)
                    nc.vector.scalar_tensor_tensor(out=sv, in0=ps[6][:, 0:P], scalar=float(D) ** -0.5, in1=blk,
                                                   op0=ALU.mult, op1=ALU.add).then_inc(z["s_read"], 1)
                    dve.wait_ge(z["s_read"], 3 * t + 1)
                    nc.vector.tensor_reduce(mx[:, t % 2, 0:1], sv, AX_X, ALU.max).then_inc(z["s_read"], 1)
                    dve.wait_ge(z["s_read"], 3 * t + 2)
                    nc.vector.tensor_scalar(sv, sv, mx[:, t % 2, 0:1], None, ALU.subtract).then_inc(z["s_read"], 1)
                if 0 <= i - 1 < TILES:
                    t = i - 1
                    dve.wait_ge(z["qkt_full"], t + 1)
                    if t >= 1:
                        dve.wait_ge(z["s_full"], t)
                    nc.vector.tensor_tensor(KT0, ps[5][:, :].rearrange("p (c r) -> p c r", c=KC),
                                            qk_w[:, 0:4].unsqueeze(2).to_broadcast([P, KC, P]), ALU.mult).then_inc(z["qkt_k"], 1)
                if 0 <= i - 2 < TILES:
                    dve.wait_ge(z["exp"], i - 1)
                    step(nc.vector.reciprocal(rc[:, i % 2, 0:1], sm[:, i % 2, 0:1]))
                    settle()
                    nc.vector.tensor_scalar(soft0[i % 2], soft0[i % 2], rc[:, i % 2, 0:1], None, ALU.mult).then_inc(z["p_ready"], 1)
                if TILES - 1 <= i < TILES + 3:
                    norm_x(1, i - TILES + 1)

            def f1_weight(i):
                part = (i - 1) // 3
                if i == 0:
                    dve.wait_ge(f1_loaded, 3 * 16)
                    step(nc.vector.tensor_scalar(nibf[0], mask8, 0.5, 0.5, ALU.mult, ALU.add))
                    settle()
                    step(nc.vector.tensor_tensor(sc_f, scale16, nibf[0], ALU.mult))
                elif i % 3 == 1:
                    if part:
                        step(nc.vector.tensor_scalar(nib, packed, 4, 15, ALU.logical_shift_right, ALU.bitwise_and))
                    else:
                        step(nc.vector.tensor_scalar(nib, packed, 15, None, ALU.bitwise_and))
                elif i % 3 == 2:
                    settle()
                    step(nc.vector.tensor_copy(nibf[part], nib))
                else:
                    settle()
                    nc.vector.scalar_tensor_tensor(out=nibf[part], in0=nibf[part], scalar=-8.0, in1=sc_f, op0=ALU.add, op1=ALU.mult)\
                        .then_inc(f1_ready, 1)

            def ffn_dve(f, phase):
                fs = ffn[f.name]
                if 0 < f.experts < 8 and not f.mix:
                    step(nc.vector.memset(lg[:, f.experts:8], -3.0e38))
                for i in range(TILES + f.next_lag + 1):
                    if 0 <= i - f.next_lag - 1 < TILES and f is not F3:
                        t = i - f.next_lag - 1
                        low_turned(phase + 1, t, rows_of(xT, t))
                    if (4 if f is F0 else 2) <= i + 1 < TILES:
                        norm_x(phase, i + 1)
                    if i < TILES and (i >= 2 or f is not F0):
                        low_turned(phase, i, rows_of(xT, i))
                    if i < 2 and f is not F0:
                        mean_var(TILES - 2 + i)
                    if (1 if f is F0 else 0) <= i - 1 < TILES and f.experts:
                        t = i - 1
                        dve.wait_ge(fs["g_full"], t + 1)
                        if t >= 2:
                            dve.wait_ge(fs["ht_full"], t - 1)
                        (gates_all if f.mix else gates_top2)(f, t, fs, ps[2 + t % 2])
                    if 0 <= i - f.add_lag < TILES:
                        t = i - f.add_lag
                        if f.bias:
                            dve.wait_ge(bias_added, t + 1 + (TILES if f is F3 else 0))
                        dve.wait_ge(fs["b_full"], t + 1)
                        nc.vector.tensor_tensor(x[:, t, :], ps[f.out_banks[t % len(f.out_banks)]][:, :], x[:, t, :], ALU.add)\
                            .then_inc(x_added, 1)
                        if f is not F3:
                            dve.wait_ge(x_added, added_before[f.name] + t + 1)
                            mean_var(t)
                    if (1 if f is F0 else 0) <= i - 1 < TILES and f.experts:
                        (weights_all if f.mix else weights_top2)(f, i - 1, fs, ps[2 + (i - 1) % 2])
                    if f is F0 and 2 <= i < 9:
                        f1_weight(i - 2)
                    if 0 <= i - f.add_lag < TILES and f is not F3:
                        norm_x(phase + 1, i - f.add_lag)

            def attend(lay, phase):
                own, per = big[lay.name]
                prime(dve, lay, "ev_dve s_read s_max s_shift s_sum s_rec p_ready o_lo normed sq_raw sq_lo")
                if lay is L1:
                    dve.wait_ge(s_mask, 32)
                    dve.wait_ge(f1_stored, 32)

                def turn(g, last):
                    def wait(name, k):
                        dve.wait_ge(own[name], done(lay, name, g, k))

                    def full(use):
                        wait("full", lay.uses.index(use) + 1)

                    def table(c, rows):
                        return cst[rows, c:c + S].unsqueeze(1).to_broadcast([rows.stop - rows.start, HALF // S, S])

                    def rope(bank, use):
                        m = lay.roped.index(use)
                        wait("roped", m - 1)
                        ta, tb = rope_terms[m % 2]
                        nc.vector.tensor_tensor(batches(ta), batches(bank[:, :]), table(C_COS, slice(0, P)), ALU.mult)
                        for lo, hi in ((0, 64), (64, 0)):
                            ins = nc.vector.tensor_tensor(batches(tb[lo:lo + 64, :]), batches(bank[hi:hi + 64, :]),
                                                          table(C_SIN, slice(hi, hi + 64)), ALU.mult)
                        ins.then_inc(own["ev_dve"], 1)

                    def empty(use):
                        kind = use[0]
                        if kind == "ss":
                            m = lay.normed.index(use)
                            wait("r_ready", m + 1)
                            r = m1_sb[:, (m % 2) * 512:(m % 2) * 512 + 512]
                            kept = place_of(use[1:])
                            if use[1] == "k":
                                ins = nc.vector.scalar_tensor_tensor(out=kept, in0=kept, scalar=qk_w[:, 4:5], in1=batches(r),
                                                                     op0=ALU.mult, op1=ALU.mult)
                            else:
                                ins = nc.vector.tensor_tensor(kept, kept, batches(r), ALU.mult)
                            ins.then_inc(own["normed"], 1)
                            return
                        if lay.norm and kind in "kq":
                            m = lay.normed.index(("ss",) + use)
                            kept = place_of(use)
                            raw = raw_squares[m % 2]
                            wait("copied", m + 1)
                            wait("sq_lo", m - 1)
                            nc.vector.tensor_tensor(batches(raw), kept, kept, ALU.mult).then_inc(own["sq_raw"], 1)
                            wait("sq_raw", m + 1)
                            wait("ev_act", lay.by_act.index(use) + 1)
                            nc.vector.tensor_tensor(squares[1], raw, squares[0].bitcast(F32), ALU.subtract)\
                                .then_inc(own["sq_lo"], 1)
                            return
                        if lay.emptier(use) != "dve":
                            return
                        full(use)
                        bank = ps[lay.bank_of[lay.uses.index(use)]]
                        if kind in "kq":
                            rope(bank, use)
                        else:
                            t = use[2]
                            if use[1]:
                                wait("ev_dve", lay.by_dve.index(("wo", use[1] - 1, t)) + 1)
                            else:
                                wait("ev_dve", lay.by_dve.index(("wo", lay.subs - 1, t)) + 1 - len(lay.by_dve))
                            nc.vector.tensor_tensor(x[:, t, :], bank[:, :], x[:, t, :], ALU.add).then_inc(own["ev_dve"], 1)

                    for sub in range(lay.subs):
                        for use in lay.pre[sub]:
                            empty(use)
                        for i in range(len(lay.fill[sub]) + 1):
                            t = sub * TILES + i
                            w = lay.keys
                            sv = s_sb[:, (t % 2) * 512:(t % 2) * 512 + 4 * w].rearrange("p (j k) -> p j k", j=4)
                            empties = lay.fill[sub][i - 1] if i >= 1 else []
                            early = [u for u in empties if u[0] in "kq"]
                            if i == 4:
                                early += [u for u in empties if u[0] == "ss"]
                            for use in early:
                                empty(use)
                            if i < TILES:
                                scores = ps[3 + t % 2][:, :].rearrange("p (j k) -> p j k", j=4)[:, :, 0:w]
                                wait("s_full", t + 1)
                                wait("t_full", t - 1)
                                if lay.wide:
                                    src = scores
                                else:
                                    pair = lambda ap: ap.rearrange("p (h b) k -> p h b k", h=2)
                                    if lay.rope:
                                        m = m1_sb[:, 2 * i * S:2 * (i + 1) * S].rearrange("p (b k) -> p b k", b=2)
                                        m = m.unsqueeze(1).to_broadcast([P, 2, 2, S])
                                        nc.vector.scalar_tensor_tensor(out=pair(sv), in0=pair(scores), scalar=float(HD) ** -0.5,
                                                                       in1=m, op0=ALU.mult, op1=ALU.add).then_inc(own["s_read"], 1)
                                    else:
                                        m = m2_sb[:, :].unsqueeze(1).to_broadcast([P, 4, S])
                                        nc.vector.scalar_tensor_tensor(out=sv, in0=scores, scalar=float(HD) ** -0.5,
                                                                       in1=m, op0=ALU.mult, op1=ALU.add).then_inc(own["s_read"], 1)
                                    wait("s_read", t + 1)
                                    src = sv
                                nc.vector.tensor_reduce(mx[:, t % 2, :], src, AX_X, ALU.max).then_inc(own["s_max"], 1)
                                wait("s_max", t + 1)
                                ins = nc.vector.tensor_tensor(sv, src, mx[:, t % 2, :].unsqueeze(2).to_broadcast([P, 4, w]), ALU.subtract)
                                ins.then_inc(own["s_shift"], 1)
                            if i >= 1:
                                for use in empties:
                                    if use not in early:
                                        empty(use)
                                    if last and use[0] == "wo" and sub == lay.subs - 1 and use[2] < TILES - 2:
                                        wait("ev_dve", lay.by_dve.index(use) + 1)
                                        mean_var(use[2])
                            if i < TILES:
                                wait("exp", t + 1)
                                nc.vector.tensor_reduce(sm[:, t % 2, :], sv, AX_X, ALU.add).then_inc(own["s_sum"], 1)
                                wait("s_sum", t + 1)
                                nc.vector.reciprocal(rc[:, t % 2, :], sm[:, t % 2, :]).then_inc(own["s_rec"], 1)
                                wait("s_rec", t + 1)
                                nc.vector.tensor_tensor(sv, sv, rc[:, t % 2, :].unsqueeze(2).to_broadcast([P, 4, w]), ALU.mult)\
                                    .then_inc(own["p_ready"], 1)
                            if 0 <= i - 2 < TILES:
                                u = t - 2
                                wait("o_hi", u + 1)
                                for b in range(2):
                                    cols = slice(b * S, (b + 1) * S)
                                    ins = nc.vector.tensor_tensor(oT[1][:, u % 4, :, cols],
                                                                  ps[6 + b][:, 0:GH * S].rearrange("p (h r) -> p h r", h=GH),
                                                                  oT[0][:, u % 4, :, cols].bitcast(F32), ALU.subtract)
                                ins.then_inc(own["o_lo"], 1)
                            if last and sub == lay.subs - 1 and i in (9, 10):
                                wait("t_full", lay.tiles)
                                norm_x(phase + 1, i - 9)

                with dve.Fori(0, lay.turns - 1) as g:
                    turn(g, False)
                turn(lay.turns - 1, True)
                dve.wait_ge(own["ev_dve"], done(lay, "ev_dve", lay.turns - 1, len(lay.by_dve)))

            ffn_dve(F0, 1)
            attend(L1, 2)
            ffn_dve(F1, 3)
            attend(L2, 4)
            ffn_dve(F2, 5)
            attend(L3, 6)
            ffn_dve(F3, 7)

        @block.tensor
        def _(pe):
            def product(dst, lhs, rhs, first, last):
                nc.tensor.matmul(dst, lhs[0], rhs[0], start=first, stop=False)
                nc.tensor.matmul(dst, lhs[0], rhs[1], start=False, stop=False)
                return nc.tensor.matmul(dst, lhs[1], rhs[0], start=False, stop=last)

            def turn(what, t, src, every_second=False):
                n = job(what, t)
                before = [m for m in range(n) if JOB_BANK[m] == JOB_BANK[n]]
                if before and n - before[-1] < 8:
                    pe.wait_ge(tr_lo, before[-1] + 1)
                for c in range(KC):
                    if every_second:
                        part = src[:, (c // 2) * 256:(c // 2 + 1) * 256].rearrange("p (r s) -> p s r", s=2)[:, c % 2, :]
                    else:
                        part = src[:, c * P:(c + 1) * P]
                    ins = nc.tensor.transpose(ps[JOB_BANK[n]][:, c * P:(c + 1) * P], part, ident)
                ins.then_inc(tr_full, 1)

            def turn_x(phase, t):
                n = XN_ORDER.index((phase, t))
                pe.wait_ge(xn_ready, n + 1)
                turn(phase, t, xn[:, n % 2, :], phase == 3)

            def rows(parts_, c, t):
                return [p[:, c, t * P:(t + 1) * P] for p in parts_]

            def l0_turns(t):
                pe.wait_ge(s_ctx[t], 16)
                turn("ctx", t, c_nat[:, t, :])
                turn_x(0, t)

            def l0_turn_feature(t):
                pe.wait_ge(z["feat"], t + 1)
                turn("feat", t, c_nat[:, t, :])

            pe.wait_ge(s_ident, 16)
            def l0_products():
                l0_turns(0)
                l0_turn_feature(0)
                for i in range(TILES + 3):
                    if i + 1 < TILES:
                        l0_turns(i + 1)
                    if i in (TILES, TILES + 1):
                        turn_x(1, i - TILES)
                    for j in range(2):
                        if i < TILES:
                            if j == 0:
                                pe.wait_ge(tr_lo, job("feat", i) + 1)
                            if j == 0:
                                pe.wait_ge(w_split, 1)
                            pe.wait_ge(dve_split, j + 1)
                            if i >= 1:
                                pe.wait_ge(z["qb"], 2 * (i - 1) + j + 1)
                            for c in range(KC):
                                lhs = rows(xT, c, i) if j == 0 else [o[:, i % 4, c, :] for o in oT]
                                w = (wq, wo)[j]
                                ins = product(ps[2 + j][:, :], lhs, [p[:, c, :] for p in w], c == 0, c == KC - 1)
                            ins.then_inc(z["qk_full"], 1)
                        if j == 0 and 0 <= i - 3 < TILES:
                            t = i - 3
                            pe.wait_ge(z["p_ready"], t + 1)
                            nc.tensor.transpose(ps[6][:, P:2 * P], soft0[t % 2], ident).then_inc(z["pt_full"], 1)
                        if j == 0 and i == TILES + 2:
                            gate_product(F0, 1, 1, W_AG0 + 1)
                    if 0 <= i - 3 < TILES:
                        t = i - 3
                        pe.wait_ge(z["pt_ready"], t + 1)
                        if t >= 1:
                            pe.wait_ge(x_added, t)
                        nc.tensor.matmul(ps[7][:, :], pt_sb[:, (t % 2) * 512:(t % 2) * 512 + P], c_nat[:, t, :], start=True, stop=True)\
                            .then_inc(z["av_full"], 1)
                    if i + 1 < TILES:
                        l0_turn_feature(i + 1)
                    if 0 <= i - 2 < TILES:
                        t = i - 2
                        pe.wait_ge(z["qkt_q"], t + 1)
                        pe.wait_ge(z["qkt_k"], t + 1)
                        if t >= 1:
                            pe.wait_ge(z["pt_ready"], t)
                        for c in range(KC):
                            ins = nc.tensor.matmul(ps[6][:, 0:P], QT0[:, c, :], KT0[:, c, :], start=(c == 0), stop=(c == KC - 1))
                        ins.then_inc(z["s_full"], 1)
                    if 0 <= i - 1 < TILES:
                        t = i - 1
                        pe.wait_ge(z["qn"], 2 * (t + 1))
                        if t >= 1:
                            pe.wait_ge(z["qkt_q"], t)
                            pe.wait_ge(z["qkt_k"], t)
                        for j in range(2):
                            for c in range(KC):
                                ins = nc.tensor.transpose(ps[4 + j][:, c * P:(c + 1) * P], qk_rows[:, t % 2, j, c * P:(c + 1) * P], ident)
                        ins.then_inc(z["qkt_full"], 1)
                    if i == TILES + 1:
                        gate_product(F0, 1, 0, W_AG0 + 1)

            def gate_product(f, phase, t, w_need):
                fs = ffn[f.name]
                pe.wait_ge(w_split, w_need)
                pe.wait_ge(tr_lo, job(phase, t) + 1)
                if t >= 2:
                    pe.wait_ge(fs["hm_ready"], t - 1)
                for c in range(KC):
                    ins = product(ps[2 + t % 2][:, 0:UPW], rows(xT, c, t), [p[:, c, 0:UPW] for p in wq], c == 0, c == KC - 1)
                ins.then_inc(fs["g_full"], 1)

            l0_products()

            def ffn_pe(f, phase, w_need, extra, before):
                fs = ffn[f.name]
                base_w = wo if f.experts else wq
                for i in range(TILES + f.next_lag):
                    if i < 2 and before:
                        last = [k for k, u in enumerate(before.uses) if before.bank_of[k] == JOB_BANK[job(phase, i)]][-1]
                        use = before.by_dve.index(before.uses[last])
                        pe.wait_ge(big[before.name][0]["ev_dve"], done(before, "ev_dve", before.turns - 1, use + 1))
                    if i < TILES and (i >= 2 or f is not F0):
                        turn_x(phase, i)
                    if 0 <= i - 1 < TILES and f.experts and (i - 1 >= 2 or f is not F0):
                        gate_product(f, phase, i - 1, w_need)
                    if 0 <= i - 2 < TILES and f.experts:
                        t = i - 2
                        pe.wait_ge(fs["hm_ready"], t + 1)
                        if t >= 1:
                            pe.wait_ge(fs["ht_ready"], t)
                        for c in range(f.chunks):
                            ins = nc.tensor.transpose(ps[6][0:f.chunk, c * P:(c + 1) * P], hm[:, t % 2, c * f.chunk:(c + 1) * f.chunk], ident)
                        ins.then_inc(fs["ht_full"], 1)
                    if 0 <= i - 3 < TILES and f.mix:
                        t = i - 3
                        pe.wait_ge(extra_loaded, extra)
                        pe.wait_ge(fs["ht_ready"], t + 1)
                        if t >= 1:
                            pe.wait_ge(fs["mx_ready"], t)
                        nc.tensor.matmul(ps[7][0:16, 0:P], cores, hT[:, t % 4, 0, :], start=True, stop=True).then_inc(fs["mx_full"], 1)
                    if 0 <= i - f.out_lag < TILES:
                        t = i - f.out_lag
                        n = len(f.out_banks)
                        if t >= n:
                            pe.wait_ge(x_added, added_before[f.name] + t - n + 1)
                        bank = ps[f.out_banks[t % n]][:, :]
                        if f.base:
                            pe.wait_ge(tr_lo, job(phase, t) + 1)
                            pe.wait_ge(w_split, w_need + (1 if f.experts else 0))
                            for c in range(KC):
                                ins = product(bank, rows(xT, c, t), [p[:, c, :] for p in base_w], c == 0, c == KC - 1 and not f.experts)
                        if f.experts:
                            pe.wait_ge(extra_loaded, extra)
                            if f.mix:
                                pe.wait_ge(fs["mx_ready"], t + 1)
                                ins = nc.tensor.matmul(bank, mT[0:16, t % 2, :], up_w[0:16, 0, :], start=False, stop=True)
                            else:
                                pe.wait_ge(fs["ht_ready"], t + 1)
                                for c in range(f.chunks):
                                    ins = nc.tensor.matmul(bank, hT[0:f.chunk, t % 4, c, :], up_w[0:f.chunk, c, :],
                                                           start=(not f.base and c == 0), stop=(c == f.chunks - 1))
                        ins.then_inc(fs["b_full"], 1)
                    if 0 <= i - f.next_lag < TILES - 2 and f is not F3:
                        turn_x(phase + 1, i - f.next_lag)

            def attend(lay, phase):
                own, per = big[lay.name]
                prime(pe, lay, "full s_full t_full o_full")
                if lay.norm:
                    pe.wait_ge(ones_ready, 1)

                def turn_heads(g, first_turn):
                    def wait(name, k):
                        pe.wait_ge(own[name], done(lay, name, g, k))

                    def emptied(use, turns_ago=0):
                        who = lay.emptier(use)
                        these = lay.by_act if who == "act" else lay.by_dve
                        wait(f"ev_{who}", these.index(use) + 1 - turns_ago * len(these))

                    def usable(use):
                        if lay.rope:
                            wait("roped", lay.roped.index(use) + 1)
                        elif lay.norm:
                            wait("normed", lay.normed.index(("ss",) + use) + 1)
                        else:
                            emptied(use)

                    def dense(use):
                        before, turn_before = lay.before(use)
                        if first_turn and turn_before:
                            turned = [m for m in range(job(phase, TILES - 2)) if JOB_BANK[m] == lay.bank_of[lay.uses.index(use)]]
                            if turned:
                                pe.wait_ge(tr_lo, turned[-1] + 1)
                        else:
                            emptied(before, int(turn_before))
                        bank = ps[lay.bank_of[lay.uses.index(use)]]
                        kind = use[0]
                        if kind in "kv":
                            src = xT if lay.wide and use[1] == 1 else cT
                            half = use[2]
                            if use == lay.uses[0]:
                                pe.wait_ge(kv_split, g + (lay.kv + 1))
                            for c in range(KC):
                                ins = product(bank[:, :], [p[:, "kv".index(kind), c, :] for p in wkv],
                                              [p[:, c, half * HALF:(half + 1) * HALF] for p in src], c == 0, c == KC - 1)
                        elif kind == "vt":
                            if lay.wide:
                                emptied(("v", 1, use[1]))
                                first = 4 * use[2]
                            else:
                                emptied(("v", 0, use[1]))
                                first = 4 * use[1]
                            for j in range(4):
                                ins = nc.tensor.transpose(bank[:, j * P:(j + 1) * P], vT_sb[:, (first + j) * P:(first + j + 1) * P], ident)
                        elif kind == "q":
                            _, sub, half, h = use
                            if half == 0 and h == 0:
                                n = g * (2 * lay.subs) + 2 * sub
                                pe.wait_ge(w_split, n + lay.w_o)
                            for c in range(KC):
                                ins = product(bank[:, :], [p[:, c, h * HD:(h + 1) * HD] for p in wq],
                                              [p[:, c, half * HALF:(half + 1) * HALF] for p in xT], c == 0, c == KC - 1)
                        elif kind == "ss":
                            m = lay.normed.index(use)
                            wait("sq_lo", m + 1)
                            nc.tensor.matmul(bank[:, :], ones_r, squares[0], start=True, stop=False)
                            ins = nc.tensor.matmul(bank[:, :], ones_r, squares[1], start=False, stop=True)
                        else:
                            _, sub, t = use
                            if t == 0:
                                n = g * (2 * lay.subs) + 2 * sub
                                pe.wait_ge(w_split, n + (lay.w_o + 1))
                            wait("o_lo", sub * TILES + t + 1)
                            for h in range(GH):
                                ins = product(bank[:, :], [o[:, t % 4, h, :] for o in oT], [p[:, h, :] for p in wo], h == 0, h == GH - 1)
                        ins.then_inc(own["full"], 1)

                    for sub in range(lay.subs):
                        for at, use in enumerate(lay.pre[sub]):
                            if first_turn and use in x_first:
                                pe.wait_ge(tr_lo, job(phase, TILES // 2 - 1 if use == x_first[0] else TILES - 1) + 1)
                            dense(use)
                            if first_turn and sub == 0 and at < 2:
                                turn_x(phase, TILES - 2 + at)
                        for i in range(len(lay.fill[sub])):
                            if i < TILES:
                                t = sub * TILES + i
                                if sub == 0 and i % 4 == 0:
                                    usable([u for u in lay.uses if u[0] == "k" and u[2] == i // 4][-1])
                                if i == 0:
                                    usable(("q", sub, 0, GH - 1))
                                if i == 4:
                                    usable(("q", sub, 1, GH - 1))
                                wait("s_read" if not lay.wide else "s_shift", t - 1)
                                for hp in range(2):
                                    for b in range(2):
                                        lhs = qT[:, 2 * i + b, 2 * hp:2 * hp + 2, :]
                                        if lay.wide:
                                            off = (2 * hp + b) * P
                                            keys = k_sb[:, (2 * i + b) * 2 * S:(2 * i + b + 1) * 2 * S]
                                        else:
                                            off = 2 * hp * P + b * S
                                            keys = k_sb[:, i * P:(i + 1) * P]
                                        ins = nc.tensor.matmul(ps[3 + t % 2][:, off:off + P], lhs, keys, start=True, stop=True)
                                ins.then_inc(own["s_full"], 1)
                            if 0 <= i - 1 < TILES:
                                t = sub * TILES + i - 1
                                wait("p_ready", t + 1)
                                wait("pt_ready", t)
                                for j in range(4 * lay.keys // P):
                                    ins = nc.tensor.transpose(ps[5][:, j * P:(j + 1) * P],
                                                              s_sb[:, (t % 2) * 512 + j * P:(t % 2) * 512 + (j + 1) * P], ident)
                                ins.then_inc(own["t_full"], 1)
                            if 0 <= i - 2 < TILES:
                                t = sub * TILES + i - 2
                                if i in (2, 6) and sub == 0:
                                    emptied([u for u in lay.uses if u[0] == "vt" and u[1] == i // 4][-1])
                                wait("pt_ready", t + 1)
                                wait("o_lo", t)
                                for b in range(2):
                                    if lay.wide:
                                        lhs = v_sb[:, (2 * (i - 2) + b) * P:(2 * (i - 2) + b + 1) * P]
                                        rhs = pt_sb[:, (t % 2) * 512:(t % 2 + 1) * 512].rearrange("p (h b r) -> p h b r", h=2, b=2)[:, :, b, :]
                                    else:
                                        lhs = v_sb[b * S:(b + 1) * S, (i - 2) * P:(i - 1) * P]
                                        rhs = pt_sb[b * S:(b + 1) * S, (t % 2) * 512:(t % 2) * 512 + 4 * S]
                                    ins = nc.tensor.matmul(ps[6 + b][:, 0:GH * S], lhs, rhs, start=True, stop=True)
                                ins.then_inc(own["o_full"], 1)
                            for use in lay.fill[sub][i]:
                                dense(use)

                of_x = [u for u in lay.uses if u[0] == "q" or (lay.wide and u[0] == "k" and u[1] == 1)]
                x_first = [[u for u in of_x if u[2] == half][0] for half in range(HALVES)]
                turn_heads(0, True)
                with pe.Fori(1, lay.turns) as g:
                    turn_heads(g, False)

            ffn_pe(F0, 1, W_AG0 + 1, 16, None)
            attend(L1, 2)
            ffn_pe(F1, 3, W_F1 + 1, 0, L1)
            attend(L2, 4)
            ffn_pe(F2, 5, W_AG2 + 1, 16 * (1 + 1 + 1), L2)
            attend(L3, 6)
            ffn_pe(F3, 7, W_AG3 + 1, 16 * (1 + 1 + 1 + 3), L3)


def kernel(**inputs):
    import concourse.bacc as bacc
    from concourse.bass_utils import run_bass_kernel_spmd

    f = {k: np.asarray(v) for k, v in inputs.items()}

    def tiles(m):
        return np.ascontiguousarray(m.reshape(TILES, P, D).transpose(1, 0, 2))

    def by_input(m):
        wide = np.zeros((D, D), m.dtype)
        wide[:, :m.shape[1]] = m
        return wide.reshape(KC, P, D).transpose(1, 0, 2).reshape(P, KC * D)

    def by_head(m):
        return m.reshape(GH, HD, D).transpose(1, 0, 2).reshape(P, GH * D)

    span = GH * HD
    qs = {1: f["L1_xattn_wq"], 2: f["L2_xattn_Wq"].T, 3: f["L3_xattn_Wq"]}
    os_ = {1: f["L1_xattn_wo"], 2: f["L2_xattn_Wo"].T, 3: f["L3_xattn_Wo"]}
    down0 = np.concatenate([f["L0_ffn_lora_A"].reshape(-1, D), f["L0_ffn_gate_W"]]).T
    down2 = np.concatenate([f["L2_ffn_A"].reshape(-1, D), f["L2_ffn_router_w"]]).T
    down3 = np.concatenate([f["L3_ffn_A_w"], f["L3_ffn_router_w"]]).T
    w = [by_input(f["L0_xattn_Wq_w"].T), by_input(down0), by_input(f["L0_ffn_base_W"].T)]
    for lay in (1, 2, 3):
        w.append(by_input(qs[lay][:, :span]))
        for n in range(GROUPS):
            w.append(by_head(os_[lay][n * span:(n + 1) * span]))
            if n + 1 < GROUPS:
                w.append(by_input(qs[lay][:, (n + 1) * span:(n + 2) * span]))
        if lay > 1:
            w.append(by_input(down2 if lay == 2 else down3))
    w.append(by_input(f["L3_ffn_W_base"].T))
    assert len(w) == W_BLOCKS - 1
    kv = []
    for k_w, v_w, heads in ((f["L1_xattn_wk"], f["L1_xattn_wv"], 8), (f["L2_xattn_Wk"].T, f["L2_xattn_Wv"].T, 8),
                            (f["L3_xattn_Wk"], f["L3_xattn_Wv"], 4)):
        for h in range(heads):
            pair = np.stack([m[:, h * HD:(h + 1) * HD].reshape(KC, P, HD) for m in (k_w, v_w)])
            kv.append(pair.transpose(2, 0, 1, 3).reshape(P, 2 * KC * HD))
    kv.append(kv[-1])

    cst = np.zeros((P, C_END), np.float32)
    cst[:, C_ID:C_ID + P] = np.eye(P)
    cst[:, C_ONE:C_ONE + P] = 1.0
    cst[:, C_BLK:C_BLK + P] = np.where(np.arange(P)[:, None] // S == np.arange(P)[None, :] // S, 0.0, NEG)
    inv = (1.0 / np.float32(10000.0) ** (np.arange(0, HD, 2, dtype=np.float32) / np.float32(HD))).astype(np.float32)
    ang = (np.arange(S, dtype=np.float32)[None, :] * inv[:, None]).astype(np.float32)
    cst[:, C_COS:C_COS + S] = np.concatenate([np.cos(ang), np.cos(ang)])
    cst[:, C_SIN:C_SIN + S] = np.concatenate([np.sin(ang), -np.sin(ang)])
    cst[:, C_IOTA:C_IOTA + 32] = np.arange(32)

    columns = [f["L0_xattn_qn_w"].reshape(KC, P).T, f["L0_xattn_kn_w"].reshape(KC, P).T,
               f["L2_xattn_q_norm_w"][:, None], f["L2_xattn_k_norm_w"][:, None]]
    m1 = f["mask_BxSxS2_ff0"].transpose(1, 0, 2).reshape(S, B * S)
    m2 = f["mask_1x1xSxS2_ff0"].reshape(S, S)
    blocks = D // 32
    packed = f["L1_ffn_weight_packed"].reshape(D, blocks * 16).T.reshape(2, P, D)
    over = lambda v: np.repeat(v.reshape(D, blocks).T, 16, axis=0).reshape(2, P, D).transpose(1, 0, 2).reshape(P, 2 * D)
    arrays = {
        "x": tiles(f["x"].reshape(ROWS, D)),
        "ctx": tiles(f["ctx_4096"].reshape(ROWS, D)),
        "w": np.stack(w),
        "kv": np.stack(kv),
        "wk": by_input(f["L0_xattn_Wk_w"].T),
        "cst": cst,
        "qkw": np.concatenate(columns, axis=1),
        "bq": f["L0_xattn_Wq_b"],
        "bk": f["L0_xattn_Wk_b"],
        "fn": f["L0_xattn_fn_w"],
        "m1": np.concatenate([m1, m1]),
        "m2": np.concatenate([m2, m2]),
        "packed": packed.transpose(1, 0, 2).reshape(P, 2 * D),
        "scale16": over(f["L1_ffn_weight_scale"]),
        "mask8": np.ascontiguousarray(over(f["L1_ffn_weight_var_mask"].view(np.uint8))).view(np.int32),
        "biasF1": f["L1_ffn_bias"],
        "biasF3": f["L3_ffn_b_base"],
        "upF0": f["L0_ffn_lora_B"].transpose(0, 2, 1).reshape(2, 112, D).transpose(1, 0, 2),
        "upF2": f["L2_ffn_B"].transpose(0, 2, 1).reshape(64, 1, D),
        "upF3": f["L3_ffn_B_w"].T.reshape(16, 1, D),
        "cores": f["L3_ffn_cores"].reshape(128, 16),
    }
    arrays = {k: np.ascontiguousarray(v) for k, v in arrays.items()}
    nc = bacc.Bacc("TRN2", target_bir_lowering=False, num_devices=1)
    aps = {k: nc.dram_tensor(f"in_{k}", v.shape, mybir.dt.from_np(v.dtype), kind="ExternalInput").ap()
           for k, v in arrays.items()}
    aps["f1_store"] = nc.dram_tensor("f1_store", (P, KC * D), F32).ap()
    out = nc.dram_tensor("out_x", (TILES, P, D), F32, kind="ExternalOutput").ap()
    build(nc, aps, out)
    r = run_bass_kernel_spmd(nc, [{f"in_{k}": v for k, v in arrays.items()}], core_ids=[0])
    return r.results[0]["out_x"].reshape(B, S, D)
```
